# Optimizing a Trainium2 kernel written in Bass

```python
import numpy as np
import jax
import jax.numpy as jnp

def _softmax(x, axis=-1):
    return jax.nn.softmax(x, axis=axis)

def _gelu(x):
    return jax.nn.gelu(x, approximate=True)

def _silu(x):
    return jax.nn.silu(x)

def _sigmoid(x):
    return jax.nn.sigmoid(x)

def _layernorm(x, axis=-1, eps=1e-05):
    m = jnp.mean(x, axis=axis, keepdims=True)
    v = jnp.var(x, axis=axis, keepdims=True)
    return (x - m) / jnp.sqrt(v + eps)

def _scatter_add(tgt, idx, src, axis=0):
    return tgt.at[idx].add(src)

def _segment_sum(src, seg, n):
    return jax.ops.segment_sum(src, seg, n)
kernel_name = 'mk_conv_preact_d2_conv_nchw64_r2_66e8d2'

def setup_inputs(seed: int=0):
    np.random.seed(seed)
    _w = jnp.asarray

    def _rec_inputs():
        import jax
        import jax.numpy as jnp
        _gk = jax.random.key(seed)
        x = -0.0003929 + 0.9999 * jax.random.normal(jax.random.fold_in(_gk, 1), (16, 32, 64, 64), jnp.float32)
        return x
    x = _rec_inputs()

    def _L0_conv_setup():
        import jax, jax.numpy as jnp
        import numpy as np
        from jax import lax
        EPS = 1e-05

        def quantize_ternary(w):
            scale = jnp.maximum(jnp.mean(jnp.abs(lax.stop_gradient(w))), EPS)
            ws = w / scale
            wq = lax.stop_gradient(jnp.clip(jnp.round(ws), -1.0, 1.0) - ws) + ws
            return wq * scale

        def conv2d(x, w, b):
            out = lax.conv_general_dilated(x, w, window_strides=(1, 1), padding=[(1, 1), (1, 1)], dimension_numbers=('NCHW', 'OIHW', 'NCHW'))
            return out + b[None, :, None, None]
        key = jax.random.key(seed)
        k1, k2, k3, k4, k5 = jax.random.split(key, 5)
        N, C_in, C_out, H, W, K = (16, 32, 32, 64, 64, 3)
        fan_in = C_in * K * K
        bound = 1.0 / np.sqrt(fan_in)
        x = jax.random.normal(k1, (N, C_in, H, W), dtype=jnp.float32)
        w = jax.random.uniform(k2, (C_out, C_in, K, K), minval=-bound, maxval=bound, dtype=jnp.float32)
        b = jax.random.uniform(k3, (C_out,), minval=-bound, maxval=bound, dtype=jnp.float32)
        w_child = jax.random.uniform(k4, (C_out, C_in, K, K), minval=-bound, maxval=bound, dtype=jnp.float32) * 0.01
        b_child = jnp.zeros((C_out,), dtype=jnp.float32)
        gate = jnp.zeros((1,), dtype=jnp.float32)
        return {'x': x, 'w': w, 'b': b, 'w_child': w_child, 'b_child': b_child, 'gate': gate}
    _L0_conv_all = _L0_conv_setup()
    _L0_conv_in = {k: v for k, v in _L0_conv_all.items() if k in ('w', 'b', 'w_child', 'b_child', 'gate')}
    del _L0_conv_all

    def _L1_conv_setup():
        import jax, jax.numpy as jnp
        import numpy as np
        K_MAX = 5
        PATCH = 4
        DIAG_EPS = 1e-05
        EPS = 1e-10

        def batch_omp(X, D):
            M, B = X.shape
            N = D.shape[1]
            G = D.T @ D + DIAG_EPS * jnp.eye(N, dtype=X.dtype)
            h_bar = (D.T @ X).T
            h = h_bar
            x_stack = None
            L = jnp.ones((B, 1, 1), X.dtype)
            I = jnp.zeros((B, 0), jnp.int32)
            mask = jnp.zeros((B, N), bool)
            bidx = jnp.arange(B)
            for k in range(1, K_MAX + 1):
                scores = jnp.abs(h * (~mask).astype(h.dtype))
                index = jnp.argmax(scores, axis=1).astype(jnp.int32)
                mask = mask.at[bidx, index].set(True)
                if k > 1:
                    G_stack = G[I, index[:, None]]
                    w = jax.scipy.linalg.solve_triangular(L, G_stack[..., None], lower=True)[..., 0]
                    w_corner = jnp.sqrt(jnp.clip(1.0 - jnp.sum(w * w, axis=1, keepdims=True), DIAG_EPS))
                    top = jnp.concatenate([L, jnp.zeros((B, k - 1, 1), X.dtype)], axis=2)
                    bot = jnp.concatenate([w, w_corner], axis=1)[:, None, :]
                    L = jnp.concatenate([top, bot], axis=1)
                I = jnp.concatenate([I, index[:, None]], axis=1)
                h_stack = jnp.take_along_axis(h_bar, I, axis=1)[..., None]
                y = jax.scipy.linalg.solve_triangular(L, h_stack, lower=True)
                x_stack = jax.scipy.linalg.solve_triangular(jnp.swapaxes(L, -1, -2), y, lower=False)[..., 0]
                beta = jnp.einsum('bk,bkn->bn', x_stack, G[I])
                h = h_bar - beta
            coeffs = jnp.zeros((B, N), X.dtype).at[bidx[:, None], I].set(x_stack)
            return coeffs.T
        key = jax.random.key(seed)
        k1, k2 = jax.random.split(key)
        z = jax.random.normal(k1, (32, 32, 64, 64), dtype=jnp.float32)
        dictionary = jax.random.normal(k2, (512, 256), dtype=jnp.float32)
        return {'z': z, 'dictionary': dictionary}
    _L1_conv_all = _L1_conv_setup()
    _L1_conv_in = {k: v for k, v in _L1_conv_all.items() if k in ('dictionary',)}
    del _L1_conv_all
    return {'x': x, 'L0_conv_w': _L0_conv_in['w'], 'L0_conv_b': _L0_conv_in['b'], 'L0_conv_w_child': _L0_conv_in['w_child'], 'L0_conv_b_child': _L0_conv_in['b_child'], 'L0_conv_gate': _L0_conv_in['gate'], 'L1_conv_dictionary': _L1_conv_in['dictionary']}

def reference(x, L0_conv_w, L0_conv_b, L0_conv_w_child, L0_conv_b_child, L0_conv_gate, L1_conv_dictionary):
    import jax
    import jax.numpy as jnp

    def _L0_conv_ref(x, w, b, w_child, b_child, gate):
        import jax, jax.numpy as jnp
        import numpy as np
        from jax import lax
        EPS = 1e-05

        def quantize_ternary(w):
            scale = jnp.maximum(jnp.mean(jnp.abs(lax.stop_gradient(w))), EPS)
            ws = w / scale
            wq = lax.stop_gradient(jnp.clip(jnp.round(ws), -1.0, 1.0) - ws) + ws
            return wq * scale

        def conv2d(x, w, b):
            out = lax.conv_general_dilated(x, w, window_strides=(1, 1), padding=[(1, 1), (1, 1)], dimension_numbers=('NCHW', 'OIHW', 'NCHW'))
            return out + b[None, :, None, None]
        out = conv2d(x, quantize_ternary(w), b)
        child_out = conv2d(x, quantize_ternary(w_child), b_child)
        g = jax.nn.sigmoid(gate)
        return out + g * child_out

    def _L1_conv_ref(z, dictionary):
        import jax, jax.numpy as jnp
        import numpy as np
        K_MAX = 5
        PATCH = 4
        DIAG_EPS = 1e-05
        EPS = 1e-10

        def batch_omp(X, D):
            M, B = X.shape
            N = D.shape[1]
            G = D.T @ D + DIAG_EPS * jnp.eye(N, dtype=X.dtype)
            h_bar = (D.T @ X).T
            h = h_bar
            x_stack = None
            L = jnp.ones((B, 1, 1), X.dtype)
            I = jnp.zeros((B, 0), jnp.int32)
            mask = jnp.zeros((B, N), bool)
            bidx = jnp.arange(B)
            for k in range(1, K_MAX + 1):
                scores = jnp.abs(h * (~mask).astype(h.dtype))
                index = jnp.argmax(scores, axis=1).astype(jnp.int32)
                mask = mask.at[bidx, index].set(True)
                if k > 1:
                    G_stack = G[I, index[:, None]]
                    w = jax.scipy.linalg.solve_triangular(L, G_stack[..., None], lower=True)[..., 0]
                    w_corner = jnp.sqrt(jnp.clip(1.0 - jnp.sum(w * w, axis=1, keepdims=True), DIAG_EPS))
                    top = jnp.concatenate([L, jnp.zeros((B, k - 1, 1), X.dtype)], axis=2)
                    bot = jnp.concatenate([w, w_corner], axis=1)[:, None, :]
                    L = jnp.concatenate([top, bot], axis=1)
                I = jnp.concatenate([I, index[:, None]], axis=1)
                h_stack = jnp.take_along_axis(h_bar, I, axis=1)[..., None]
                y = jax.scipy.linalg.solve_triangular(L, h_stack, lower=True)
                x_stack = jax.scipy.linalg.solve_triangular(jnp.swapaxes(L, -1, -2), y, lower=False)[..., 0]
                beta = jnp.einsum('bk,bkn->bn', x_stack, G[I])
                h = h_bar - beta
            coeffs = jnp.zeros((B, N), X.dtype).at[bidx[:, None], I].set(x_stack)
            return coeffs.T
        'Patch-wise OMP sparse coding bottleneck (forward reconstruction path).\n            z: [B, C, H, W]; dictionary: [atom_dim, num_embeddings], atom_dim = C*PATCH^2.\n            '
        D = dictionary / (jnp.linalg.norm(dictionary, axis=0, keepdims=True) + EPS)
        B, C, H, W = z.shape
        p = PATCH
        hb, wb = (H // p, W // p)
        patches = z.reshape(B, C, hb, p, wb, p).transpose(0, 2, 4, 1, 3, 5).reshape(B * hb * wb, C * p * p)
        X = patches.T
        coeffs = batch_omp(X, D)
        X_hat = D @ coeffs
        recon = X_hat.T.reshape(B, hb, wb, C, p, p).transpose(0, 3, 1, 4, 2, 5).reshape(B, C, H, W)
        return recon

    def _gn(v, G=32, eps=1e-05):
        B_, C_, H_, W_ = v.shape
        g = v.reshape(B_, G, C_ // G, H_, W_)
        m = jnp.mean(g, axis=(2, 3, 4), keepdims=True)
        s = jnp.var(g, axis=(2, 3, 4), keepdims=True)
        return ((g - m) / jnp.sqrt(s + eps)).reshape(v.shape)

    def _ln_c(v, eps=1e-06):
        m = jnp.mean(v, axis=1, keepdims=True)
        s = jnp.var(v, axis=1, keepdims=True)
        return (v - m) / jnp.sqrt(s + eps)

    def _ln_t(v, eps=1e-05):
        m = jnp.mean(v, axis=-1, keepdims=True)
        s = jnp.var(v, axis=-1, keepdims=True)
        return (v - m) / jnp.sqrt(s + eps)

    def _to_tokens(v):
        B_, C_, H_, W_ = v.shape
        return v.reshape(B_, C_, H_ * W_).transpose(0, 2, 1)

    def _from_tokens(t, like):
        B_, C_, H_, W_ = like.shape
        return t.transpose(0, 2, 1).reshape(B_, C_, H_, W_)
    x = x + _L0_conv_ref(_gn(x), L0_conv_w, L0_conv_b, L0_conv_w_child, L0_conv_b_child, L0_conv_gate)
    x = x + _L1_conv_ref(_gn(x), L1_conv_dictionary)
    return x

_drawn_inputs = setup_inputs


def setup_inputs(seed=0):
    import zlib

    import numpy as np

    out = dict(_drawn_inputs(seed))
    spreads = {'L0_conv_b_child': (0.0, 0.1)}
    factors = {'L0_conv_w_child': 3.877}
    for name, (base, spread) in spreads.items():
        noise = np.random.default_rng([zlib.crc32(name.encode()), seed]).standard_normal(out[name].shape)
        drawn = base * np.exp(spread * noise) if base else spread * noise
        out[name] = jnp.asarray(drawn.astype(out[name].dtype))
    for name, factor in factors.items():
        out[name] = (out[name] * factor).astype(out[name].dtype)
    return out
```

```python
import numpy as np
import concourse.bass as bass
import concourse.mybir as mybir
from contextlib import ExitStack

F32 = mybir.dt.float32
BF16 = mybir.dt.bfloat16
U32 = mybir.dt.uint32
ALU = mybir.AluOpType
ACT = mybir.ActivationFunctionType
AX = mybir.AxisListType


def build_program(nc, x_in, w_in, b_in, wc_in, bc_in, gate_in, dict_in, out):
    IMAGES, C, H, W = x_in.shape
    P = 128
    ATOM_DIM, ATOMS = dict_in.shape
    PATCH = 4
    GR = H // PATCH
    PIX = GR * W
    PAD_W = W + 2
    STEPS = 5
    IMG_R = 4
    ROUNDS = IMAGES // IMG_R
    TILES = 4
    CHUNKS = ATOMS // P
    TAPS = 9
    HALF = PIX // 2
    GN_EPS = 1e-5
    DIAG_EPS = 1e-5
    SCALE_EPS = 1e-5
    NORM_EPS = 1e-10
    JUNK = 6

    ctx = ExitStack()
    with ctx:
        def sb(name, shape, dt=F32):
            return ctx.enter_context(nc.sbuf_tensor(name, shape, dt))

        def sem(name):
            return ctx.enter_context(nc.semaphore(name))

        gram_dram = nc.dram_tensor("gram", [ATOMS, ATOMS], F32, kind="Internal").ap()

        ident = sb("ident", [P, P])
        ones = sb("ones", [P, P])
        same_channel = sb("same_channel", [P, P])
        center = sb("center", [P, P])
        iota = sb("iota", [P, ATOMS])
        rank = sb("rank", [P, 8])
        w_taps = sb("w_taps", [P, 3, P])
        w_mid = sb("w_mid", [P, IMG_R, P])
        w_sum = sb("w_sum", [P, 2])
        w_scale = sb("w_scale", [P, 4])
        gate = sb("gate", [P, 2])
        b_raw = sb("b_raw", [P, 2])
        b_eff = sb("b_eff", [P, 1])
        d_sb = sb("d_sb", [P, PATCH, ATOMS])
        d_t = sb("d_t", [P, CHUNKS, PATCH, P])
        xa = sb("xa", [P, IMG_R, GR + 1, PAD_W])
        bn_x = sb("bn_x", [P, IMG_R, 3, 6])
        bn_1 = sb("bn_1", [P, IMG_R, 2, 6])
        st_x = sb("st_x", [P, IMG_R, 2])
        st_1 = sb("st_1", [P, IMG_R, 2])
        gn = sb("gn", [P, 2, 12, IMG_R])
        x1 = sb("x1", [P, IMAGES, PIX])
        z = sb("z", [P, IMG_R, PIX])
        score = [sb(f"score{s}", [P, TILES, ATOMS]) for s in range(2)]
        rows = [sb(f"rows{s}", [P, STEPS - 1, TILES, ATOMS]) for s in range(2)]
        diag = [sb(f"diag{s}", [P, TILES, STEPS - 1, P]) for s in range(2)]
        junk = sb("junk", [P, JUNK, ATOMS], BF16)
        top = [sb(f"top{s}", [P, TILES, 8]) for s in range(2)]
        top_i = [sb(f"top_i{s}", [P, TILES, 8], U32) for s in range(2)]
        enc = [sb(f"enc{s}", [P, TILES, 8]) for s in range(2)]
        free = [sb(f"free{s}", [P, TILES, 8, STEPS - 1]) for s in range(2)]
        keep = [sb(f"keep{s}", [P, TILES, 8]) for s in range(2)]
        best = [sb(f"best{s}", [P, TILES], U32) for s in range(2)]
        idx_u = [sb(f"idx_u{s}", [P, STEPS, TILES], U32) for s in range(2)]
        idx = [sb(f"idx{s}", [P, TILES, STEPS]) for s in range(2)]
        h_at = [sb(f"h_at{s}", [P, TILES]) for s in range(2)]
        g_at = [sb(f"g_at{s}", [P, TILES, STEPS - 1]) for s in range(2)]
        n_inv = [sb(f"n_inv{s}", [P, TILES, STEPS, STEPS]) for s in range(2)]
        prod = [sb(f"prod{s}", [P, TILES, STEPS - 1, STEPS - 1]) for s in range(2)]
        w_vec = [sb(f"w_vec{s}", [P, TILES, STEPS - 1]) for s in range(2)]
        a_vec = [sb(f"a_vec{s}", [P, TILES, STEPS - 1]) for s in range(2)]
        aw = [sb(f"aw{s}", [P, TILES, STEPS - 1]) for s in range(2)]
        d_neg = [sb(f"d_neg{s}", [P, TILES]) for s in range(2)]
        d_k = [sb(f"d_k{s}", [P, TILES]) for s in range(2)]
        rd = [sb(f"rd{s}", [P, TILES, STEPS]) for s in range(2)]
        c_neg = [sb(f"c_neg{s}", [P, TILES]) for s in range(2)]
        dx = [sb(f"dx{s}", [P, TILES, STEPS]) for s in range(2)]
        x_neg = [sb(f"x_neg{s}", [P, TILES, STEPS]) for s in range(2)]
        picked = sb("picked", [P, TILES, STEPS, ATOMS])
        coef_t = sb("coef_t", [P, CHUNKS, 2 * P])
        y = sb("y", [P, 2, PIX])
        w_raw = z[:, 0, 0:2 * C * TAPS].rearrange("p (i n) -> p i n", i=2)
        w_tmp = z[:, 1, 0:3 * C * TAPS].rearrange("p (i n) -> p i n", i=3)
        d_tmp = y[:, 0, :].rearrange("p (c a) -> p c a", a=ATOMS)
        d_norm = y[:, 1, :].rearrange("p (c a) -> p c a", a=ATOMS)
        w_t = z[:, 2, 0:TAPS * C].rearrange("p (t c) -> p t c", c=C)
        gram = coef_t[:, :, :]
        iota_i = junk[:, 0:2, :].rearrange("p a n -> p (a n)").bitcast(U32)

        h = [ctx.enter_context(nc.psum_tensor(f"h{s}", [P, TILES, ATOMS], F32)) for s in range(2)]
        conv_ps = ctx.enter_context(nc.psum_tensor("conv_ps", [P, 2, HALF], F32))
        back_ps = [ctx.enter_context(nc.psum_tensor(f"back_ps{b}", [P, 2, 2 * P], F32)) for b in range(2)]

        const_done = sem("const_done")
        w_loaded = sem("w_loaded")
        d_loaded = sem("d_loaded")
        pads_zero = sem("pads_zero")
        w_sum_ready = sem("w_sum_ready")
        w_sum_ps = sem("w_sum_ps")
        gate_done = sem("gate_done")
        w_ready = sem("w_ready")
        d_sq = sem("d_sq")
        d_sq_ps = sem("d_sq_ps")
        d_nrm = sem("d_nrm")
        d_root = sem("d_root")
        d_ready = sem("d_ready")
        d_t_ps = sem("d_t_ps")
        d_t_done = sem("d_t_done")
        gram_ps = sem("gram_ps")
        gram_sb_done = sem("gram_sb_done")
        gram_stored = sem("gram_stored")
        x_loaded = [sem(f"x_loaded{m}") for m in range(IMG_R)]
        x_stats = sem("x_stats")
        x_stats_ps = sem("x_stats_ps")
        x_var = sem("x_var")
        x_root = sem("x_root")
        x_params = sem("x_params")
        x_normed = sem("x_normed")
        conv_in = sem("conv_in")
        conv_turn = sem("conv_turn")
        conv_done = sem("conv_done")
        x1_done = sem("x1_done")
        y_stats = sem("y_stats")
        y_stats_ps = sem("y_stats_ps")
        y_var = sem("y_var")
        y_root = sem("y_root")
        y_params = sem("y_params")
        z_done = sem("z_done")
        h_ready = [sem(f"h_ready{s}") for s in range(2)]
        score_ready = [sem(f"score_ready{s}") for s in range(2)]
        idx_ready = [sem(f"idx_ready{s}") for s in range(2)]
        rows_in = [[sem(f"rows_in{s}_{j}") for j in range(STEPS - 1)] for s in range(2)]
        dx_ready = [sem(f"dx_ready{s}") for s in range(2)]
        diag_ready = [sem(f"diag_ready{s}") for s in range(2)]
        h_read = [sem(f"h_read{s}") for s in range(2)]
        picked_ready = sem("picked_ready")
        coef_ready = sem("coef_ready")
        coef_t_ps = sem("coef_t_ps")
        coef_t_done = sem("coef_t_done")
        recon_ps = sem("recon_ps")
        y_done = sem("y_done")
        y_stored = [sem(f"y_stored{m}") for m in range(IMG_R)]
        dve_step = sem("dve_step")
        pool_step = sem("pool_step")
        act_step = sem("act_step")

        block = ctx.enter_context(nc.Block())

        held = {eng: sem(f"held_{name}") for name, eng in (('pool', nc.gpsimd), ('pe', nc.tensor), ('act', nc.scalar), ('dve', nc.vector))}

        def hold(eng, signal, value):
            eng.wait_ge(signal, value)
            eng.sem_inc(held[eng], 1)

        @block.sync
        def _(sp):
            for i, (w_d, b_d) in enumerate([(w_in, b_in), (wc_in, bc_in)]):
                for q in range(PATCH):
                    part = slice(q * C, (q + 1) * C)
                    sp.dma_start(w_raw[part, i, :], w_d.rearrange("o i a b -> o (i a b)")).then_inc(w_loaded, 16)
                    sp.dma_start(b_raw[part, i:i + 1], b_d.rearrange("(o i) -> o i", i=1)).then_inc(w_loaded, 16)
            sp.dma_start(gate[:, 0:1], gate_in.rearrange("(a b) -> a b", a=1).to_broadcast([P, 1])).then_inc(w_loaded, 16)

            def load(f, m):
                if isinstance(f, int):
                    src = x_in[IMG_R * f + m]
                else:
                    src = x_in[bass.ds(IMG_R * f + m, 1)].rearrange("a c r w -> (a c) r w")
                sp.dma_start(xa[0:C, m, 1:GR + 1, 1:W + 1], src[:, PATCH - 1:H:PATCH, :]).then_inc(x_loaded[m], 16)
                for q in range(1, PATCH):
                    sp.dma_start(xa[q * C:(q + 1) * C, m, 0:GR, 1:W + 1],
                                 src[:, q - 1:H:PATCH, :]).then_inc(x_loaded[m], 16)

            for m in range(IMG_R):
                sp.sem_inc(y_stored[m], 16 * PATCH)
            sp.wait_ge(pads_zero, 1)
            load(0, 0)
            load(0, 1)
            d_view = dict_in.rearrange("(c r x) a -> r c (x a)", r=PATCH, x=PATCH)
            for q in range(PATCH):
                sp.dma_start(d_sb[q * C:(q + 1) * C, :, :].rearrange("p x a -> p (x a)"), d_view[q]).then_inc(d_loaded, 16)
            load(0, 2)
            load(0, 3)
            sp.wait_ge(gram_sb_done, 1)
            sp.dma_start(gram_dram.rearrange("(k p) a -> p k a", p=P), gram[:, :, :]).then_inc(gram_stored, 16)

            def loads_ahead(f):
                for m in range(IMG_R):
                    sp.wait_ge(conv_done, 2 * (IMG_R * (f - 1) + m) + 2)
                    load(f, m)

            def stores(r):
                for m in range(IMG_R):
                    sp.wait_ge(y_done, 2 * (IMG_R * r + m) + 4)
                    if isinstance(r, int):
                        dst = out[IMG_R * r + m]
                    else:
                        dst = out[bass.ds(IMG_R * r + m, 1)].rearrange("a c r w -> (a c) r w")
                    for q in range(PATCH):
                        sp.dma_start(dst[:, q:H:PATCH, :],
                                     y[q * C:(q + 1) * C, m % 2, :].rearrange("p (g w) -> p g w", w=W)).then_inc(y_stored[m], 16)

            loads_ahead(1)
            with sp.Fori(0, ROUNDS - 2) as r:
                loads_ahead(r + 2)
                stores(r)
            stores(ROUNDS - 2)
            stores(ROUNDS - 1)
            for m in range(IMG_R):
                sp.wait_ge(y_stored[m], 16 * PATCH * (ROUNDS + 1))

        @block.gpsimd
        def _(pool):
            n = 0

            def step(ins):
                nonlocal n
                n += 1
                ins.then_inc(pool_step, 1)
                pool.wait_ge(pool_step, n)

            step(nc.gpsimd.memset(ident[:, :], 0.0))
            step(nc.gpsimd.memset(same_channel[:, :], 0.0))
            step(nc.gpsimd.memset(center[:, :], 0.0))
            step(nc.gpsimd.memset(ones[:, :], 1.0))
            step(nc.gpsimd.iota(iota_i[:, :], pattern=[[1, ATOMS]], base=0, channel_multiplier=0))

            def put_ones(t, offset):
                step(nc.gpsimd.affine_select(out=t[:, :], in_=t[:, :], compare_op=ALU.not_equal, fill=1.0,
                                             base=-offset, pattern=[[1, P]], channel_multiplier=-1))

            put_ones(ident, 0)
            for q in range(1 - PATCH, PATCH):
                put_ones(same_channel, q * C)
            put_ones(center, -C)
            put_ones(center, P - C)
            nc.gpsimd.tensor_copy(iota[:, :], iota_i[:, :]).then_inc(const_done, 1)

            def gather(r, s, k):
                hold(pool, idx_ready[s], (STEPS - 1) * r + k + 1)
                for t in range(TILES):
                    pool.indirect_dma_start(out=rows[s][:, k, t, :], out_offset=None, in_=gram_dram[:, :],
                                            in_offset=bass.IndirectOffsetOnAxis(ap=idx_u[s][:, k, t:t + 1], axis=0)
                                            ).then_inc(rows_in[s][k], 16)

            pool_base = n

            def sum_picked(r, s):
                for t in range(TILES):
                    i = 4 * (TILES * s + t)
                    pool.wait_ge(picked_ready, TILES * (2 * r + s) + t + 1)
                    base = pool_base + 8 * 4 * r + i
                    nc.gpsimd.tensor_tensor(picked[:, t, 0, :], picked[:, t, 0, :], picked[:, t, 1, :], ALU.add).then_inc(pool_step, 1)
                    nc.gpsimd.tensor_tensor(picked[:, t, 2, :], picked[:, t, 2, :], picked[:, t, 3, :], ALU.add).then_inc(pool_step, 1)
                    pool.wait_ge(pool_step, base + 2)
                    nc.gpsimd.tensor_tensor(picked[:, t, 0, :], picked[:, t, 0, :], picked[:, t, 2, :], ALU.add).then_inc(pool_step, 1)
                    pool.wait_ge(pool_step, base + 3)
                    nc.gpsimd.tensor_tensor(picked[:, t, 0, :], picked[:, t, 0, :], picked[:, t, 4, :], ALU.add).then_inc(pool_step, 1)
                    pool.wait_ge(pool_step, base + 4)
                    pool.sem_inc(coef_ready, 1)

            pool.wait_ge(gram_stored, 16)

            def body(r):
                for k in range(STEPS - 1):
                    for s in range(2):
                        gather(r, s, k)
                for s in range(2):
                    sum_picked(r, s)

            with pool.Fori(0, ROUNDS) as r:
                body(r)

        @block.tensor
        def _(pe):
            def mm(dst, lhs, rhs, start, stop, skip=False):
                return nc.tensor.matmul(dst, lhs, rhs, start=start, stop=stop, skip_group_check=skip)

            pe.sem_inc(coef_t_ps, 1)
            pe.wait_ge(const_done, 1)
            pe.wait_ge(w_sum_ready, 1)
            mm(conv_ps[:, 0, 0:2], ones[:, :], w_sum[:, :], True, True).then_inc(w_sum_ps, 1)
            pe.wait_ge(d_sq, 1)
            for c in range(PATCH):
                last = mm(conv_ps[:, 1, 0:ATOMS], ones[:, :], d_tmp[:, c, :], c == 0, c == PATCH - 1)
            last.then_inc(d_sq_ps, 1)
            def x_sums(f):
                pe.wait_ge(x_stats, f + 1)
                mm(conv_ps[:, 0, 0:2 * IMG_R], same_channel[:, :], st_x[:, :, :].rearrange("p m a -> p (m a)"),
                   True, True).then_inc(x_stats_ps, 1)

            pe.wait_ge(w_ready, 1)
            x_sums(0)
            pe.wait_ge(d_ready, 1)
            for k in range(CHUNKS):
                for c in range(PATCH):
                    last = nc.tensor.transpose(back_ps[k][:, c // 2, c % 2 * P:(c % 2 + 1) * P],
                                               d_sb[:, c, k * P:(k + 1) * P], ident[:, :])
            last.then_inc(d_t_ps, 1)
            for k in range(CHUNKS):
                for c in range(PATCH):
                    last = mm(h[0][:, 2 * k, :], d_sb[:, c, k * P:(k + 1) * P], d_sb[:, c, :], c == 0, c == PATCH - 1)
            last.then_inc(gram_ps, 1)

            def y_sums(f):
                pe.wait_ge(y_stats, f + 1)
                mm(conv_ps[:, 0, 0:2 * IMG_R], same_channel[:, :], st_1[:, :, :].rearrange("p m a -> p (m a)"),
                   True, True).then_inc(y_stats_ps, 1)

            def conv(f, m):
                hold(pe, conv_in, IMG_R * f + m + 1)
                if not (isinstance(f, int) and f == 0 and m == 0):
                    hold(pe, x1_done, 2 * (IMG_R * f + m))
                lo, hi = slice(0, P // 2), slice(P // 2, P)
                for turn in range(2):
                    for i, kx in enumerate((0, 2, 1)):
                        wk = w_mid[:, m, :] if kx == 1 else w_taps[:, kx, :]
                        blocks = [(lo, lo, turn, 0), (lo, hi, turn, 1), (hi, lo, 1 - turn, 0), (hi, hi, 1 - turn, 0)]
                        for rows_in_, rows_out, b, shift in blocks:
                            g0 = b * GR // 2 + shift
                            last = mm(conv_ps[rows_out, b, :], wk[rows_in_, rows_out],
                                      xa[rows_in_, m, g0:g0 + GR // 2, kx:kx + W],
                                      i == 0 and turn == 0, i == 2 and turn == 1, True)
                    if turn == 0:
                        last.then_inc(conv_turn, 1)
                        hold(pe, conv_turn, IMG_R * f + m + 1)
                last.then_inc(conv_done, 2)

            def correlate(f, s):
                pe.wait_ge(z_done, IMG_R * f + 2 * s + 2)
                if not (isinstance(f, int) and f == 0):
                    pe.wait_ge(h_read[s], STEPS * f)
                for t in range(TILES):
                    zt = z[:, 2 * s + t // 2, t % 2 * HALF:(t % 2 + 1) * HALF].rearrange("p (n c) -> p c n", c=PATCH)
                    for c in range(PATCH):
                        last = mm(h[s][:, t, :], zt[:, c, :], d_sb[:, c, :], t % 2 == 0 and c == 0, c == PATCH - 1, True)
                    if t % 2:
                        last.then_inc(h_ready[s], 1)

            def update(r, s, k):
                pe.wait_ge(rows_in[s][k], 16 * TILES * (r + 1))
                for t in range(TILES):
                    pe.wait_ge(diag_ready[s], TILES * (r * (STEPS - 1) + k) + t + 1)
                    for j in range(k + 1):
                        last = mm(h[s][:, t, :], diag[s][:, t, j, :], rows[s][:, j, t, :], False, j == k, True)
                    if t % 2:
                        last.then_inc(h_ready[s], 1)

            def back(r, s):
                for i in range(2):
                    m = 2 * s + i
                    n = IMG_R * r + m
                    pe.wait_ge(coef_ready, TILES * (2 * r + s) + 2 * i + 2)
                    pe.wait_ge(y_done, 2 * n + 2)
                    for k in range(CHUNKS):
                        for t in range(2):
                            last = nc.tensor.transpose(back_ps[0][:, k, t * P:(t + 1) * P],
                                                       picked[:, 2 * i + t, 0, k * P:(k + 1) * P], ident[:, :])
                    last.then_inc(coef_t_ps, 1)
                    pe.wait_ge(coef_t_done, n + 1)
                    for half in (1, 0):
                        for c2 in range(2):
                            c = 2 * half + c2
                            if isinstance(n, int):
                                res = x1[:, n, c:PIX:PATCH]
                            else:
                                res = x1[:, bass.ds(n, 1), c:PIX:PATCH].rearrange("p a n -> p (a n)")
                            mm(back_ps[half][:, c2, :], ident[:, :], res, c2 == 0, False, True)
                            for k in range(CHUNKS):
                                last = mm(back_ps[half][:, c2, :], d_t[:, k, c, :], coef_t[:, k, :], False,
                                          k == CHUNKS - 1, True)
                        last.then_inc(recon_ps, 1)

            for m in range(IMG_R):
                conv(0, m)
            y_sums(0)
            pe.wait_ge(gram_sb_done, 1)
            pe.wait_ge(d_t_done, 1)
            for s in range(2):
                correlate(0, s)

            def body(r, front):
                f = r + 1
                update(r, 0, 0)
                update(r, 1, 0)
                if front:
                    x_sums(f)
                m = 0
                for k in (1, 2):
                    for s in range(2):
                        update(r, s, k)
                        if front:
                            conv(f, m)
                        m += 1
                update(r, 0, 3)
                if front:
                    y_sums(f)
                update(r, 1, 3)
                if front:
                    for s in range(2):
                        correlate(f, s)
                for s in range(2):
                    back(r, s)

            with pe.Fori(0, ROUNDS - 1) as r:
                body(r, True)
            body(ROUNDS - 1, False)

        @block.scalar
        def _(act):
            act.wait_ge(w_loaded, 16 * (4 * PATCH + 1))
            nc.scalar.activation(gate[:, 1:2], gate[:, 0:1], ACT.Sigmoid).then_inc(gate_done, 1)
            act.wait_ge(d_loaded, 16 * PATCH)
            nc.scalar.activation(d_tmp[:, :, :], d_sb[:, :, :], ACT.Square).then_inc(d_sq, 1)
            act.wait_ge(d_nrm, 1)
            nc.scalar.activation(d_norm[:, 1, :], d_norm[:, 0, :], ACT.Sqrt).then_inc(d_root, 1)

            def root(ready, done, which, f):
                act.wait_ge(ready, f + 1)
                nc.scalar.activation(gn[:, which, 5, :], gn[:, which, 4, :], ACT.Sqrt).then_inc(done, 1)

            def norm_x(f, m):
                if m == 0:
                    act.wait_ge(x_params, f + 1)
                nc.scalar.activation(xa[:, m, :, 1:W + 1], xa[:, m, :, 1:W + 1], ACT.Identity,
                                     bias=gn[:, 0, 9, m:m + 1], scale=gn[:, 0, 8, m:m + 1]).then_inc(x_normed, 1)

            def image_of(t, n):
                return t[:, n, :] if isinstance(n, int) else t[:, bass.ds(n, 1), :].rearrange("p a n -> p (a n)")

            def out_conv(f, m):
                n = IMG_R * f + m
                hold(act, conv_done, 2 * n + 2)
                for b in range(2):
                    nc.scalar.activation(image_of(x1, n)[:, b * HALF:(b + 1) * HALF], conv_ps[:, b, :], ACT.Identity,
                                         bias=gn[:, 0, 10, m:m + 1]).then_inc(x1_done, 1)

            def norm_y(f, m):
                n = IMG_R * f + m
                if m == 0:
                    act.wait_ge(y_params, f + 1)
                    act.wait_ge(x1_done, 2 * IMG_R * (f + 1))
                    if not (isinstance(f, int) and f == 0):
                        hold(act, h_ready[1], 2 * STEPS * (f - 1) + 2)
                nc.scalar.activation(z[:, m, :], image_of(x1, n), ACT.Identity,
                                     bias=gn[:, 1, 9, m:m + 1], scale=gn[:, 1, 8, m:m + 1]).then_inc(z_done, 1)

            def scores(r, s, k):
                for b in range(2):
                    act.wait_ge(h_ready[s], 2 * (STEPS * r + k) + b + 1)
                    if b == 0 and not (isinstance(r, int) and r == 0 and k == 0):
                        act.wait_ge(h_read[s], STEPS * r + k)
                    nc.scalar.activation(score[s][:, 2 * b:2 * b + 2, :], h[s][:, 2 * b:2 * b + 2, :], ACT.Abs
                                         ).then_inc(score_ready[s], 1)

            def diags(r, s, k):
                act.wait_ge(dx_ready[s], (STEPS - 1) * r + k + 1)
                if not (isinstance(r, int) and r == 0 and k == 0):
                    act.wait_ge(h_ready[s], 2 * (STEPS * r + k) + 2)
                for t in range(TILES):
                    for j in range(k + 1):
                        last = nc.scalar.activation(diag[s][:, t, j, :], ident[:, :], ACT.Copy, scale=dx[s][:, t, j:j + 1])
                    last.then_inc(diag_ready[s], 1)

            def out_back(r, s):
                for i in range(2):
                    n = IMG_R * r + 2 * s + i
                    act.wait_ge(coef_t_ps, n + 2)
                    nc.scalar.activation(coef_t[:, :, :], back_ps[0][:, :, :], ACT.Copy, scale=-1.0).then_inc(coef_t_done, 1)
                    act.wait_ge(y_stored[2 * (1 - s) + i], 16 * PATCH * (r + s + 1))
                    for q, half in enumerate((1, 0)):
                        act.wait_ge(recon_ps, 2 * n + q + 1)
                        nc.scalar.activation(y[:, i, :].rearrange("p (n c) -> p c n", c=PATCH)[:, 2 * half:2 * half + 2, :],
                                             back_ps[half][:, :, :], ACT.Copy).then_inc(y_done, 1)

            act.sem_inc(y_done, 2)
            root(x_var, x_root, 0, 0)
            act.wait_ge(d_t_ps, 1)
            for k in range(CHUNKS):
                last = nc.scalar.activation(d_t[:, k, :, :].rearrange("p c n -> p (c n)"),
                                            back_ps[k][:, :, :].rearrange("p a n -> p (a n)"), ACT.Copy)
            last.then_inc(d_t_done, 1)
            for m in range(IMG_R):
                norm_x(0, m)
            for m in range(IMG_R):
                out_conv(0, m)
            root(y_var, y_root, 1, 0)
            for m in range(IMG_R):
                norm_y(0, m)
            for s in range(2):
                scores(0, s, 0)

            def body(r, front):
                f = r + 1
                diags(r, 0, 0)
                diags(r, 1, 0)
                scores(r, 0, 1)
                if front:
                    root(x_var, x_root, 0, f)
                scores(r, 1, 1)
                diags(r, 0, 1)
                if front:
                    norm_x(f, 0)
                    norm_x(f, 1)
                diags(r, 1, 1)
                scores(r, 0, 2)
                if front:
                    out_conv(f, 0)
                scores(r, 1, 2)
                if front:
                    norm_x(f, 2)
                    norm_x(f, 3)
                diags(r, 0, 2)
                if front:
                    out_conv(f, 1)
                diags(r, 1, 2)
                scores(r, 0, 3)
                if front:
                    out_conv(f, 2)
                scores(r, 1, 3)
                diags(r, 0, 3)
                if front:
                    out_conv(f, 3)
                diags(r, 1, 3)
                scores(r, 0, 4)
                if front:
                    root(y_var, y_root, 1, f)
                scores(r, 1, 4)
                if front:
                    for m in range(IMG_R):
                        norm_y(f, m)
                    scores(f, 0, 0)
                    scores(f, 1, 0)
                out_back(r, 0)
                out_back(r, 1)

            with act.Fori(0, ROUNDS - 1) as r:
                body(r, True)
            body(ROUNDS - 1, False)

        @block.vector
        def _(dve):
            v = nc.vector
            n = 0

            def step(ins):
                nonlocal n
                n += 1
                return ins.then_inc(dve_step, 1)

            def sync():
                dve.wait_ge(dve_step, n)

            def restart():
                nonlocal n
                sync()
                dve.sem_clear(dve_step)
                n = 0

            for m in range(IMG_R):
                step(v.memset(xa[:, m, :, :], 0.0))
            sync()
            dve.sem_inc(pads_zero, 1)
            for c in range(8):
                step(v.memset(rank[:, c:c + 1], 1024.0 * (8 - c)))
            for s in range(2):
                step(v.memset(n_inv[s][:, :, :, :], 0.0))
                step(v.memset(rd[s][:, :, :], 1.0))
            sync()
            for s in range(2):
                for k in range(STEPS):
                    step(v.memset(n_inv[s][:, :, k, k:k + 1], 1.0))
            step(v.memset(w_taps[:, :, :], 0.0))

            def x_statistics(f, m):
                dve.wait_ge(x_loaded[m], 16 * PATCH * (f + 1))
                g = 0
                for i, rows_ in enumerate((6, 6, 5)):
                    step(v.bn_stats(out=bn_x[:, m, i, :], in_=xa[:, m, g:g + rows_, 1:W + 1]))
                    g += rows_
                sync()
                step(v.bn_aggr(out=st_x[:, m, :], in_=bn_x[:, m, :, :]))

            def to_moments(st, done, which):
                sync()
                step(v.tensor_tensor(gn[:, which, 0, :], st[:, :, 0], st[:, :, 0], ALU.mult))
                sync()
                n_before = n
                step(v.tensor_tensor(st[:, :, 1], st[:, :, 1], gn[:, which, 0, :], ALU.add))
                sync()
                dve.sem_inc(done, 1)

            def variance(f, which, sums, done, count):
                g = gn[:, which]
                dve.wait_ge(sums, f + 1)
                step(v.tensor_scalar(g[:, 1:3, :], conv_ps[:, 0, 0:2 * IMG_R].rearrange("p (m a) -> p a m", a=2),
                                     count / (H * W), None, ALU.mult))
                sync()
                step(v.tensor_tensor(g[:, 3, :], g[:, 1, :], g[:, 1, :], ALU.mult))
                sync()
                step(v.tensor_tensor(g[:, 3, :], g[:, 2, :], g[:, 3, :], ALU.subtract))
                sync()
                v.tensor_scalar(g[:, 4, :], g[:, 3, :], 0.0, GN_EPS, ALU.max, ALU.add).then_inc(done, 1)

            def norm_params(f, which, root_done, done):
                g = gn[:, which]
                dve.wait_ge(root_done, f + 1)
                step(v.reciprocal(g[:, 6, :], g[:, 5, :]))
                sync()
                step(v.tensor_tensor(g[:, 6, :], g[:, 6, :], g[:, 4, :], ALU.mult))
                sync()
                step(v.tensor_tensor(g[:, 7, :], g[:, 5, :], g[:, 6, :], ALU.add))
                sync()
                step(v.tensor_scalar(g[:, 7, :], g[:, 7, :], 0.5, None, ALU.mult))
                sync()
                step(v.reciprocal(g[:, 8, :], g[:, 7, :]))
                step(v.tensor_scalar(g[:, 10, :], g[:, 1, :], b_eff[:, 0:1], None, ALU.add))
                sync()
                v.scalar_tensor_tensor(out=g[:, 9, :], in0=g[:, 1, :], scalar=-1.0, in1=g[:, 8, :],
                                       op0=ALU.mult, op1=ALU.mult).then_inc(done, 1)

            def conv_operands(f, m):
                dve.wait_ge(x_normed, IMG_R * f + m + 1)
                step(v.memset(xa[0:C, m, 0, 1:W + 1], 0.0))
                step(v.memset(xa[C:2 * C, m, GR, 1:W + 1], 0.0))
                step(v.memset(xa[2 * C:3 * C, m, GR, 1:W + 1], 0.0))
                step(v.memset(xa[3 * C:4 * C, m, GR, 1:W + 1], 0.0))
                step(v.scalar_tensor_tensor(out=w_mid[:, m, :], in0=center[:, :], scalar=gn[:, 0, 7, m:m + 1],
                                            in1=w_taps[:, 1, :], op0=ALU.mult, op1=ALU.add))
                sync()
                dve.sem_inc(conv_in, 1)

            def y_statistics(f, m):
                n_img = IMG_R * f + m
                dve.wait_ge(x1_done, 2 * n_img + 2)
                src = x1[:, n_img, :] if isinstance(n_img, int) else x1[:, bass.ds(n_img, 1), :].rearrange("p a n -> p (a n)")
                for b in range(2):
                    step(v.bn_stats(out=bn_1[:, m, b, :], in_=src[:, b * HALF:(b + 1) * HALF]))
                sync()
                step(v.bn_aggr(out=st_1[:, m, :], in_=bn_1[:, m, :, :]))

            def scan(r, s, k):
                for t in range(TILES):
                    if t % 2 == 0:
                        hold(dve, score_ready[s], 2 * (STEPS * r + k) + t // 2 + 1)
                    step(v.max(out=top[s][:, t, :], in_=score[s][:, t, :]))
                for t in range(TILES):
                    dve.wait_ge(dve_step, n - TILES + 1)
                    step(v.max_index(out=top_i[s][:, t, :], in_max=top[s][:, t, :], in_values=score[s][:, t, :]))

            def select(r, s, k):
                sync()
                if k == 0:
                    step(v.memset(x_neg[s][:, :, 1:STEPS], 0.0))
                    step(v.tensor_copy(idx_u[s][:, 0, :], top_i[s][:, :, 0]))
                    step(v.tensor_copy(idx[s][:, :, 0], top_i[s][:, :, 0]))
                    sync()
                else:
                    by_rank = rank[:, :].rearrange("p (a c) -> p a c", a=1).to_broadcast([P, TILES, 8])
                    step(v.tensor_tensor(enc[s][:, :, :], top_i[s][:, :, :], by_rank, ALU.add))
                    if k == 1:
                        step(v.tensor_tensor(keep[s][:, :, :], top_i[s][:, :, :],
                                             idx[s][:, :, 0:1].to_broadcast([P, TILES, 8]), ALU.not_equal))
                    else:
                        i8 = top_i[s][:, :, :].rearrange("p t (c a) -> p t c a", a=1).to_broadcast([P, TILES, 8, k])
                        old = idx[s][:, :, 0:k].rearrange("p t (a j) -> p t a j", a=1).to_broadcast([P, TILES, 8, k])
                        step(v.tensor_tensor(free[s][:, :, :, 0:k], i8, old, ALU.not_equal))
                        sync()
                        step(v.tensor_reduce(keep[s][:, :, :], free[s][:, :, :, 0:k], AX.X, ALU.min))
                    sync()
                    step(v.tensor_tensor(enc[s][:, :, :], enc[s][:, :, :], keep[s][:, :, :], ALU.mult))
                    sync()
                    step(v.tensor_reduce(best[s][:, :], enc[s][:, :, :], AX.X, ALU.max))
                    sync()
                    step(v.tensor_scalar(idx_u[s][:, k, :], best[s][:, :], 1023, None, ALU.bitwise_and))
                    sync()
                    step(v.tensor_copy(idx[s][:, :, k], idx_u[s][:, k, :]))
                    sync()
                if k < STEPS - 1:
                    dve.sem_inc(idx_ready[s], 1)

            def pick(s, t, k, source, dst):
                if junk_n[0] >= JUNK:
                    dve.wait_ge(dve_step, n - JUNK + 1)
                junk_n[0] += 1
                step(v.scalar_tensor_tensor(out=junk[:, junk_n[0] % JUNK, :], in0=iota[:, :], scalar=idx[s][:, t, k:k + 1],
                                            in1=source, op0=ALU.is_equal, op1=ALU.mult, accum_out=dst))

            junk_n = [0]

            def extract(r, s, k):
                for t in range(TILES):
                    pick(s, t, k, h[s][:, t, :], h_at[s][:, t:t + 1])
                for j in range(k):
                    if j == k - 1:
                        dve.wait_ge(rows_in[s][j], 16 * TILES * (r + 1))
                    for t in range(TILES):
                        pick(s, t, k, rows[s][:, j, t, :], g_at[s][:, t, j:j + 1])
                sync()
                dve.sem_inc(h_read[s], 1)

            def solve(r, s, k):
                T = TILES
                if k > 0:
                    g_b = g_at[s][:, :, 0:k].rearrange("p t (a j) -> p t a j", a=1).to_broadcast([P, T, k, k])
                    step(v.tensor_tensor(prod[s][:, :, 0:k, 0:k], n_inv[s][:, :, 0:k, 0:k], g_b, ALU.mult))
                    sync()
                    step(v.tensor_reduce(w_vec[s][:, :, 0:k], prod[s][:, :, 0:k, 0:k], AX.X, ALU.add))
                    sync()
                    step(v.tensor_tensor(a_vec[s][:, :, 0:k], w_vec[s][:, :, 0:k], rd[s][:, :, 0:k], ALU.mult))
                    sync()
                    step(v.tensor_tensor(aw[s][:, :, 0:k], a_vec[s][:, :, 0:k], w_vec[s][:, :, 0:k], ALU.mult))
                    a_b = a_vec[s][:, :, 0:k].rearrange("p t (a i) -> p t a i", a=1).to_broadcast([P, T, k, k])
                    step(v.tensor_tensor(prod[s][:, :, 0:k, 0:k],
                                         n_inv[s][:, :, 0:k, 0:k].rearrange("p t i j -> p t j i"), a_b, ALU.mult))
                    sync()
                    step(v.tensor_reduce(d_neg[s][:, :], aw[s][:, :, 0:k], AX.X, ALU.add, negate=True))
                    step(v.tensor_reduce(n_inv[s][:, :, k, 0:k], prod[s][:, :, 0:k, 0:k], AX.X, ALU.add, negate=True))
                    sync()
                    step(v.tensor_scalar(d_k[s][:, :], d_neg[s][:, :], 1.0, DIAG_EPS, ALU.add, ALU.max))
                    sync()
                    step(v.reciprocal(rd[s][:, :, k], d_k[s][:, :]))
                    sync()
                step(v.scalar_tensor_tensor(out=c_neg[s][:, :], in0=h_at[s][:, :], scalar=-1.0, in1=rd[s][:, :, k],
                                            op0=ALU.mult, op1=ALU.mult))
                sync()
                c_b = c_neg[s][:, :].rearrange("p (t a) -> p t a", a=1).to_broadcast([P, T, k + 1])
                step(v.tensor_tensor(dx[s][:, :, 0:k + 1], n_inv[s][:, :, k, 0:k + 1], c_b, ALU.mult))
                sync()
                if k < STEPS - 1:
                    dve.sem_inc(dx_ready[s], 1)
                if k == 0:
                    step(v.tensor_copy(x_neg[s][:, :, 0], dx[s][:, :, 0]))
                else:
                    step(v.tensor_tensor(x_neg[s][:, :, 0:k + 1], x_neg[s][:, :, 0:k + 1], dx[s][:, :, 0:k + 1], ALU.add))

            def scatter(r, s):
                sync()
                for t in range(TILES):
                    if t % 2 == 0:
                        dve.wait_ge(coef_t_ps, IMG_R * r + 1 + (0 if s == 0 else t // 2 + 1))
                    for j in range(STEPS):
                        last = step(v.tensor_scalar(picked[:, t, j, :], iota[:, :], idx[s][:, t, j:j + 1],
                                                    x_neg[s][:, t, j:j + 1], ALU.is_equal, ALU.mult))
                    sync()
                    dve.sem_inc(picked_ready, 1)

            dve.wait_ge(w_loaded, 16 * (4 * PATCH + 1))
            step(v.tensor_reduce(w_sum[:, :], w_raw[:, :, :], AX.X, ALU.add, apply_absolute_value=True))
            sync()
            dve.sem_inc(w_sum_ready, 1)
            for m in range(IMG_R):
                x_statistics(0, m)
            to_moments(st_x, x_stats, 0)
            dve.wait_ge(w_sum_ps, 1)
            step(v.tensor_scalar(w_scale[:, 0:2], conv_ps[:, 0, 0:2], 1.0 / (PATCH * C * C * TAPS), SCALE_EPS, ALU.mult, ALU.max))
            sync()
            step(v.tensor_scalar(w_scale[:, 2:4], w_scale[:, 0:2], 0.5, None, ALU.mult))
            dve.wait_ge(gate_done, 1)
            sync()
            for i in range(2):
                step(v.tensor_scalar(w_tmp[:, 0, :], w_raw[:, i, :], w_scale[:, 2 + i:3 + i], w_scale[:, i:i + 1], ALU.is_gt, ALU.mult))
                step(v.tensor_scalar(w_tmp[:, 1, :], w_raw[:, i, :], -1.0, w_scale[:, 2 + i:3 + i], ALU.mult, ALU.is_gt))
                sync()
                step(v.tensor_scalar(w_tmp[:, 1, :], w_tmp[:, 1, :], w_scale[:, i:i + 1], None, ALU.mult))
                sync()
                step(v.tensor_tensor(w_raw[:, i, :], w_tmp[:, 0, :], w_tmp[:, 1, :], ALU.subtract))
                sync()
            step(v.scalar_tensor_tensor(out=w_tmp[:, 2, :], in0=w_raw[:, 1, :], scalar=gate[:, 1:2], in1=w_raw[:, 0, :],
                                        op0=ALU.mult, op1=ALU.add))
            step(v.scalar_tensor_tensor(out=b_eff[:, :], in0=b_raw[:, 1:2], scalar=gate[:, 1:2], in1=b_raw[:, 0:1],
                                        op0=ALU.mult, op1=ALU.add))
            sync()
            for tap in range(TAPS):
                step(v.transpose(w_t[:, tap, :], w_tmp[:, 2, :].rearrange("p (i t) -> p t i", t=TAPS)[:, tap, :]))
            sync()
            for q in range(PATCH):
                for p in range(PATCH):
                    ky = (q - p) % PATCH
                    if ky < 3:
                        part = slice(q * C, (q + 1) * C)
                        step(v.tensor_copy(w_taps[part, :, p * C:(p + 1) * C], w_t[part, 3 * ky:3 * ky + 3, :]))
            sync()
            dve.sem_inc(w_ready, 1)
            dve.wait_ge(const_done, 1)
            variance(0, 0, x_stats_ps, x_var, 1.0 * (GR + 1) * W)
            dve.wait_ge(d_sq_ps, 1)
            step(v.tensor_copy(d_norm[:, 0, :], conv_ps[:, 1, 0:ATOMS]))
            sync()
            dve.sem_inc(d_nrm, 1)
            norm_params(0, 0, x_root, x_params)
            dve.wait_ge(d_root, 1)
            step(v.reciprocal(d_norm[:, 2, :], d_norm[:, 1, :]))
            sync()
            step(v.tensor_tensor(d_norm[:, 3, :], d_norm[:, 2, :], d_norm[:, 0, :], ALU.mult))
            sync()
            step(v.tensor_tensor(d_norm[:, 2, :], d_norm[:, 3, :], d_norm[:, 1, :], ALU.add))
            sync()
            step(v.tensor_scalar(d_norm[:, 3, :], d_norm[:, 2, :], 0.5, NORM_EPS, ALU.mult, ALU.add))
            sync()
            step(v.reciprocal(d_norm[:, 2, :], d_norm[:, 3, :]))
            sync()
            for c in range(PATCH):
                step(v.tensor_tensor(d_sb[:, c, :], d_sb[:, c, :], d_norm[:, 2, :], ALU.mult))
            sync()
            dve.sem_inc(d_ready, 1)
            for m in range(IMG_R):
                conv_operands(0, m)
            dve.wait_ge(gram_ps, 1)
            for k in range(CHUNKS):
                step(v.tensor_copy(gram[:, k, :], h[0][:, 2 * k, :]))
            sync()
            for k in range(CHUNKS):
                step(v.scalar_tensor_tensor(out=gram[:, k, k * P:(k + 1) * P], in0=ident[:, :], scalar=DIAG_EPS,
                                            in1=gram[:, k, k * P:(k + 1) * P], op0=ALU.mult, op1=ALU.add))
            sync()
            dve.sem_inc(gram_sb_done, 1)
            for m in range(IMG_R):
                y_statistics(0, m)
            to_moments(st_1, y_stats, 1)
            variance(0, 1, y_stats_ps, y_var, 1.0 * PIX)
            norm_params(0, 1, y_root, y_params)

            def body(r, front):
                f = r + 1
                restart()
                junk_n[0] = 0
                scan(r, 0, 0)
                select(r, 0, 0)
                scan(r, 1, 0)
                extract(r, 0, 0)
                solve(r, 0, 0)
                select(r, 1, 0)
                extract(r, 1, 0)
                solve(r, 1, 0)
                if front:
                    for m in range(IMG_R):
                        x_statistics(f, m)
                    to_moments(st_x, x_stats, 0)
                for k in range(1, STEPS):
                    scan(r, 0, k)
                    if front and k == 1:
                        variance(f, 0, x_stats_ps, x_var, 1.0 * (GR + 1) * W)
                    if front and k == 4:
                        variance(f, 1, y_stats_ps, y_var, 1.0 * PIX)
                    select(r, 0, k)
                    if front and k == 2:
                        y_statistics(f, 0)
                    scan(r, 1, k)
                    if front and k == 1:
                        norm_params(f, 0, x_root, x_params)
                    if front and k == 2:
                        conv_operands(f, 2)
                        conv_operands(f, 3)
                    if front and k == 3:
                        y_statistics(f, 2)
                    extract(r, 0, k)
                    if front and k == 4:
                        norm_params(f, 1, y_root, y_params)
                    solve(r, 0, k)
                    if front and k == 2:
                        y_statistics(f, 1)
                    if front and k == 3:
                        y_statistics(f, 3)
                        to_moments(st_1, y_stats, 1)
                    if k == STEPS - 1:
                        scatter(r, 0)
                    select(r, 1, k)
                    extract(r, 1, k)
                    if front and k == 1:
                        conv_operands(f, 0)
                        conv_operands(f, 1)
                    solve(r, 1, k)
                    if k == STEPS - 1:
                        scatter(r, 1)

            with dve.Fori(0, ROUNDS - 1) as r:
                body(r, True)
            body(ROUNDS - 1, False)


_INS = ['x', 'L0_conv_w', 'L0_conv_b', 'L0_conv_w_child', 'L0_conv_b_child', 'L0_conv_gate', 'L1_conv_dictionary']


def kernel(**inputs):
    import numpy as _np
    import concourse.bacc as _bacc
    from concourse import mybir as _mybir
    from concourse.bass_utils import run_bass_kernel_spmd as _run

    nc = _bacc.Bacc("TRN2", target_bir_lowering=False, num_devices=1)
    arrays, args = {}, []
    for name in _INS:
        a = _np.ascontiguousarray(inputs[name])
        arrays[f"in_{name}"] = a
        args.append(nc.dram_tensor(f"in_{name}", a.shape, _mybir.dt.from_np(a.dtype), kind="ExternalInput").ap())
    result = nc.dram_tensor("out_0", inputs['x'].shape, _mybir.dt.float32, kind="ExternalOutput").ap()
    build_program(nc, *args, result)
    r = _run(nc, [arrays], core_ids=[0])
    return r.results[0]["out_0"]
```

```python
import numpy as np
import concourse.bass as bass
import concourse.mybir as mybir
from contextlib import ExitStack

F32 = mybir.dt.float32
BF16 = mybir.dt.bfloat16
U32 = mybir.dt.uint32
ALU = mybir.AluOpType
ACT = mybir.ActivationFunctionType
AX = mybir.AxisListType


def build_program(nc, x_in, w_in, b_in, wc_in, bc_in, gate_in, dict_in, out):
    IMAGES, C, H, W = x_in.shape
    P = 128
    ATOM_DIM, ATOMS = dict_in.shape
    PATCH = 4
    GR = H // PATCH
    PIX = GR * W
    PAD_W = W + 2
    STEPS = 5
    IMG_R = 4
    ROUNDS = IMAGES // IMG_R
    TILES = 4
    CHUNKS = ATOMS // P
    TAPS = 9
    HALF = PIX // 2
    GN_EPS = 1e-5
    DIAG_EPS = 1e-5
    SCALE_EPS = 1e-5
    NORM_EPS = 1e-10
    JUNK = 6

    ctx = ExitStack()
    with ctx:
        def sb(name, shape, dt=F32):
            return ctx.enter_context(nc.sbuf_tensor(name, shape, dt))

        def sem(name):
            return ctx.enter_context(nc.semaphore(name))

        gram_dram = nc.dram_tensor("gram", [ATOMS, ATOMS], F32, kind="Internal").ap()

        ident = sb("ident", [P, P])
        ones = sb("ones", [P, P])
        same_channel = sb("same_channel", [P, P])
        center = sb("center", [P, P])
        iota = sb("iota", [P, ATOMS])
        rank = sb("rank", [P, 8])
        w_taps = sb("w_taps", [P, 3, P])
        w_mid = sb("w_mid", [P, IMG_R, P])
        w_sum = sb("w_sum", [P, 2])
        w_scale = sb("w_scale", [P, 4])
        gate = sb("gate", [P, 2])
        b_raw = sb("b_raw", [P, 2])
        b_eff = sb("b_eff", [P, 1])
        d_sb = sb("d_sb", [P, PATCH, ATOMS])
        d_t = sb("d_t", [P, CHUNKS, PATCH, P])
        xa = sb("xa", [P, IMG_R, GR + 1, PAD_W])
        sum_x = sb("sum_x", [P, 2, IMG_R])
        sum_1 = sb("sum_1", [P, 3, IMG_R])
        gn = sb("gn", [P, 2, 12, IMG_R])
        xb = sb("xb", [P, 2, GR, PAD_W])
        x1 = sb("x1", [P, IMAGES, PIX])
        z = sb("z", [P, IMG_R, PIX])
        score = [sb(f"score{s}", [P, TILES, ATOMS]) for s in range(2)]
        rows = [sb(f"rows{s}", [P, STEPS - 1, TILES, ATOMS]) for s in range(2)]
        diag = [sb(f"diag{s}", [P, TILES, STEPS - 1, P]) for s in range(2)]
        junk = sb("junk", [P, JUNK, ATOMS], BF16)
        top = [sb(f"top{s}", [P, TILES, 8]) for s in range(2)]
        top_i = [sb(f"top_i{s}", [P, TILES, 8], U32) for s in range(2)]
        enc = [sb(f"enc{s}", [P, TILES, 8]) for s in range(2)]
        free = [sb(f"free{s}", [P, TILES, 8, STEPS - 1]) for s in range(2)]
        keep = [sb(f"keep{s}", [P, TILES, 8]) for s in range(2)]
        best = [sb(f"best{s}", [P, TILES], U32) for s in range(2)]
        idx_u = [sb(f"idx_u{s}", [P, STEPS, TILES], U32) for s in range(2)]
        idx = [sb(f"idx{s}", [P, TILES, STEPS]) for s in range(2)]
        h_at = [sb(f"h_at{s}", [P, TILES]) for s in range(2)]
        g_at = [sb(f"g_at{s}", [P, TILES, STEPS - 1]) for s in range(2)]
        n_inv = [sb(f"n_inv{s}", [P, TILES, STEPS, STEPS]) for s in range(2)]
        prod = [sb(f"prod{s}", [P, TILES, STEPS - 1, STEPS - 1]) for s in range(2)]
        w_vec = [sb(f"w_vec{s}", [P, TILES, STEPS - 1]) for s in range(2)]
        a_vec = [sb(f"a_vec{s}", [P, TILES, STEPS - 1]) for s in range(2)]
        aw = [sb(f"aw{s}", [P, TILES, STEPS - 1]) for s in range(2)]
        d_neg = [sb(f"d_neg{s}", [P, TILES]) for s in range(2)]
        d_k = [sb(f"d_k{s}", [P, TILES]) for s in range(2)]
        rd = [sb(f"rd{s}", [P, TILES, STEPS]) for s in range(2)]
        c_neg = [sb(f"c_neg{s}", [P, TILES]) for s in range(2)]
        dx = [sb(f"dx{s}", [P, TILES, STEPS]) for s in range(2)]
        x_neg = [sb(f"x_neg{s}", [P, TILES, STEPS]) for s in range(2)]
        x_last = [sb(f"x_last{s}", [P, TILES, STEPS]) for s in range(2)]
        idx_last = [sb(f"idx_last{s}", [P, TILES, STEPS]) for s in range(2)]
        picked = sb("picked", [P, 2, 2, STEPS, ATOMS])
        coef_t = sb("coef_t", [P, CHUNKS, 2 * P])
        spare = picked[:, :, :, :, :].rearrange("p a b j n -> p (a b) (j n)")
        w_raw = spare[:, 0, 0:2 * C * TAPS].rearrange("p (i n) -> p i n", i=2)
        w_tmp = spare[:, 1, 0:3 * C * TAPS].rearrange("p (i n) -> p i n", i=3)
        d_tmp = x1[:, IMAGES - 1, :].rearrange("p (c a) -> p c a", a=ATOMS)
        d_norm = x1[:, IMAGES - 2, :].rearrange("p (c a) -> p c a", a=ATOMS)
        w_t = spare[:, 2, 0:TAPS * C].rearrange("p (t c) -> p t c", c=C)
        gram = coef_t[:, :, :]
        unread = z[:, 0:2, :].rearrange("p m n -> p (m n)").bitcast(BF16)[:, 0:3 * (GR + 1) * W].rearrange(
            "p (a g w) -> p a g w", a=3, w=W)
        iota_i = junk[:, 0:2, :].rearrange("p a n -> p (a n)").bitcast(U32)

        h = [ctx.enter_context(nc.psum_tensor(f"h{s}", [P, TILES, ATOMS], F32)) for s in range(2)]
        conv_ps = ctx.enter_context(nc.psum_tensor("conv_ps", [P, 2, HALF], F32))
        back_ps = [ctx.enter_context(nc.psum_tensor(f"back_ps{b}", [P, 2, 2 * P], F32)) for b in range(2)]

        const_done = sem("const_done")
        w_loaded = sem("w_loaded")
        d_loaded = sem("d_loaded")
        pads_zero = sem("pads_zero")
        w_sum_ready = sem("w_sum_ready")
        w_sum_ps = sem("w_sum_ps")
        gate_done = sem("gate_done")
        w_ready = sem("w_ready")
        d_sq = sem("d_sq")
        d_sq_ps = sem("d_sq_ps")
        d_nrm = sem("d_nrm")
        d_root = sem("d_root")
        d_ready = sem("d_ready")
        d_t_ps = sem("d_t_ps")
        d_t_done = sem("d_t_done")
        gram_ps = sem("gram_ps")
        gram_sb_done = sem("gram_sb_done")
        gram_stored = sem("gram_stored")
        xa_loaded = [sem(f"xa_loaded{m}") for m in range(IMG_R)]
        xb_loaded = [sem(f"xb_loaded{m}") for m in range(2)]
        x_stats = sem("x_stats")
        x_stats_ps = sem("x_stats_ps")
        x_var = sem("x_var")
        x_root = sem("x_root")
        x_params = sem("x_params")
        x_normed = sem("x_normed")
        w_mid_ready = sem("w_mid_ready")
        conv_done = sem("conv_done")
        x1_done = sem("x1_done")
        y_stats = sem("y_stats")
        y_stats_ps = sem("y_stats_ps")
        y_var = sem("y_var")
        y_root = sem("y_root")
        y_params = sem("y_params")
        z_done = sem("z_done")
        h_ready = [sem(f"h_ready{s}") for s in range(2)]
        score_ready = [sem(f"score_ready{s}") for s in range(2)]
        idx_ready = [sem(f"idx_ready{s}") for s in range(2)]
        rows_in = [[sem(f"rows_in{s}_{j}") for j in range(STEPS - 1)] for s in range(2)]
        dx_ready = [sem(f"dx_ready{s}") for s in range(2)]
        diag_ready = [sem(f"diag_ready{s}") for s in range(2)]
        h_read = [sem(f"h_read{s}") for s in range(2)]
        picked_ready = sem("picked_ready")
        coef_ready = sem("coef_ready")
        coef_t_ps = sem("coef_t_ps")
        coef_t_done = sem("coef_t_done")
        recon_ps = sem("recon_ps")
        y_done = sem("y_done")
        y_stored = sem("y_stored")
        dve_step = sem("dve_step")
        pool_step = sem("pool_step")
        act_step = sem("act_step")

        block = ctx.enter_context(nc.Block())

        held = {eng: sem(f"held_{name}") for name, eng in (('pool', nc.gpsimd), ('pe', nc.tensor), ('act', nc.scalar), ('dve', nc.vector))}

        def hold(eng, signal, value):
            eng.wait_ge(signal, value)
            eng.sem_inc(held[eng], 1)

        @block.sync
        def _(sp):
            for i, (w_d, b_d) in enumerate([(w_in, b_in), (wc_in, bc_in)]):
                for q in range(PATCH):
                    part = slice(q * C, (q + 1) * C)
                    sp.dma_start(w_raw[part, i, :], w_d.rearrange("o i a b -> o (i a b)")).then_inc(w_loaded, 16)
                    sp.dma_start(b_raw[part, i:i + 1], b_d.rearrange("(o i) -> o i", i=1)).then_inc(w_loaded, 16)
            sp.dma_start(gate[:, 0:1], gate_in.rearrange("(a b) -> a b", a=1).to_broadcast([P, 1])).then_inc(w_loaded, 16)

            def source(n):
                return x_in[n] if isinstance(n, int) else x_in[bass.ds(n, 1)].rearrange("a c r w -> (a c) r w")

            def load_a(n, m):
                src = source(n)
                for q in range(PATCH - 1):
                    sp.dma_start(xa[q * C:(q + 1) * C, m, 0:GR, 1:W + 1], src[:, q:H:PATCH, :]).then_inc(xa_loaded[m], 16)
                sp.dma_start(xa[3 * C:4 * C, m, 1:GR + 1, 1:W + 1], src[:, PATCH - 1:H:PATCH, :]).then_inc(xa_loaded[m], 16)

            def load_b(n, m):
                src = source(n)
                for q in range(PATCH - 1):
                    sp.dma_start(xb[q * C:(q + 1) * C, m % 2, 0:GR, 1:W + 1], src[:, q + 1:H:PATCH, :]).then_inc(xb_loaded[m % 2], 16)
                sp.dma_start(xb[3 * C:4 * C, m % 2, 0:GR - 1, 1:W + 1], src[:, PATCH:H:PATCH, :]).then_inc(xb_loaded[m % 2], 16)

            sp.wait_ge(pads_zero, 1)
            load_a(0, 0)
            load_a(1, 1)
            d_view = dict_in.rearrange("(c r x) a -> r c (x a)", r=PATCH, x=PATCH)
            for q in range(PATCH):
                sp.dma_start(d_sb[q * C:(q + 1) * C, :, :].rearrange("p x a -> p (x a)"), d_view[q]).then_inc(d_loaded, 16)
            load_a(2, 2)
            load_a(3, 3)
            load_b(0, 0)
            load_b(1, 1)
            sp.wait_ge(gram_sb_done, 1)
            sp.dma_start(gram_dram.rearrange("(k p) a -> p k a", p=P), gram[:, :, :]).then_inc(gram_stored, 16)

            def loads_ahead(f, more=True):
                for m in range(IMG_R):
                    n = IMG_R * f + m
                    if more or m + 2 < IMG_R:
                        sp.wait_ge(conv_done, 2 * n + 2)
                        load_b(n + 2, m)
                    if more:
                        load_a(n + IMG_R, m)

            def store(r, m):
                n = IMG_R * r + m
                sp.wait_ge(y_done, 2 * n + 4)
                dst = out[n] if isinstance(n, int) else out[bass.ds(n, 1)].rearrange("a c r w -> (a c) r w")
                for q in range(PATCH):
                    part = slice(q * C, (q + 1) * C)
                    src = x1[part, n, :] if isinstance(n, int) else x1[part, bass.ds(n, 1), :].rearrange("p a n -> p (a n)")
                    sp.dma_start(dst[:, q:H:PATCH, :], src.rearrange("p (g w) -> p g w", w=W)).then_inc(y_stored, 16)

            def body(r, front, more, behind):
                if behind:
                    store(r - 1, 0)
                if front:
                    loads_ahead(r + 1, more)
                if behind:
                    for m in range(1, IMG_R):
                        store(r - 1, m)

            loads_ahead(0)
            body(0, True, True, False)
            with sp.Fori(1, ROUNDS - 2) as r:
                body(r, True, True, True)
            body(ROUNDS - 2, True, False, True)
            body(ROUNDS - 1, False, False, True)
            for m in range(IMG_R):
                store(ROUNDS - 1, m)
            sp.wait_ge(y_stored, 16 * PATCH * IMAGES)

        @block.gpsimd
        def _(pool):
            n = 0

            def step(ins):
                nonlocal n
                n += 1
                ins.then_inc(pool_step, 1)
                pool.wait_ge(pool_step, n)

            step(nc.gpsimd.memset(ident[:, :], 0.0))
            step(nc.gpsimd.memset(same_channel[:, :], 0.0))
            step(nc.gpsimd.memset(center[:, :], 0.0))
            step(nc.gpsimd.memset(ones[:, :], 1.0))
            step(nc.gpsimd.iota(iota_i[:, :], pattern=[[1, ATOMS]], base=0, channel_multiplier=0))

            def put_ones(t, offset):
                step(nc.gpsimd.affine_select(out=t, in_=t, compare_op=ALU.not_equal, fill=1.0,
                                             base=-offset, pattern=[[1, t.shape[1]]], channel_multiplier=-1))

            put_ones(ident[:, :], 0)
            for q in range(1 - PATCH, PATCH):
                put_ones(same_channel[:, :], q * C)
            put_ones(center[:, 0:P // 2], 0)
            put_ones(center[:, P // 2:P], -C)
            nc.gpsimd.tensor_copy(iota[:, :], iota_i[:, :]).then_inc(const_done, 1)

            def gather(r, s, k):
                hold(pool, idx_ready[s], (STEPS - 1) * r + k + 1)
                for t in range(TILES):
                    pool.indirect_dma_start(out=rows[s][:, k, t, :], out_offset=None, in_=gram_dram[:, :],
                                            in_offset=bass.IndirectOffsetOnAxis(ap=idx_u[s][:, k, t:t + 1], axis=0)
                                            ).then_inc(rows_in[s][k], 16)

            pool.wait_ge(gram_stored, 16)

            pool_base = n

            def sum_picked(r, m):
                for t in range(2):
                    hold(pool, picked_ready, 2 * (IMG_R * r + m) + t + 1)
                    for j in range(1, STEPS):
                        last = nc.gpsimd.tensor_tensor(picked[:, m % 2, t, 0, :], picked[:, m % 2, t, 0, :],
                                                       picked[:, m % 2, t, j, :], ALU.add)
                        if j < STEPS - 1:
                            count = pool_base + 2 * (STEPS - 2) * (IMG_R * r + m) + (STEPS - 2) * t + j
                            last.then_inc(pool_step, 1)
                            hold(pool, pool_step, count)
                    last.then_inc(coef_ready, 1)

            def body(r, behind):
                for k in range(STEPS - 1):
                    for s in range(2):
                        gather(r, s, k)
                        if behind and (s, k) == (0, 2):
                            sum_picked(r - 1, 2)
                if behind:
                    sum_picked(r - 1, 3)
                sum_picked(r, 0)
                sum_picked(r, 1)

            body(0, False)
            with pool.Fori(1, ROUNDS) as r:
                body(r, True)
            sum_picked(ROUNDS - 1, 2)
            sum_picked(ROUNDS - 1, 3)

        @block.tensor
        def _(pe):
            def mm(dst, lhs, rhs, start, stop, skip=False):
                return nc.tensor.matmul(dst, lhs, rhs, start=start, stop=stop, skip_group_check=skip)

            pe.sem_inc(coef_t_ps, 2)
            pe.wait_ge(const_done, 1)
            pe.wait_ge(w_sum_ready, 1)
            mm(conv_ps[:, 0, 0:2], ones[:, :], w_sum[:, :], True, True).then_inc(w_sum_ps, 1)
            pe.wait_ge(d_sq, 1)
            for c in range(PATCH):
                last = mm(conv_ps[:, 1, 0:ATOMS], ones[:, :], d_tmp[:, c, :], c == 0, c == PATCH - 1)
            last.then_inc(d_sq_ps, 1)
            def x_sums(f):
                pe.wait_ge(x_stats, 2 * IMG_R * (f + 1))
                mm(conv_ps[:, 0, 0:2 * IMG_R], same_channel[:, :], sum_x[:, :, :].rearrange("p a m -> p (a m)"),
                   True, True).then_inc(x_stats_ps, 1)

            pe.wait_ge(w_ready, 1)
            x_sums(0)
            pe.wait_ge(d_ready, 1)
            for k in range(CHUNKS):
                for c in range(PATCH):
                    last = nc.tensor.transpose(back_ps[k][:, c // 2, c % 2 * P:(c % 2 + 1) * P],
                                               d_sb[:, c, k * P:(k + 1) * P], ident[:, :])
            last.then_inc(d_t_ps, 1)
            for k in range(CHUNKS):
                for c in range(PATCH):
                    last = mm(h[0][:, 2 * k, :], d_sb[:, c, k * P:(k + 1) * P], d_sb[:, c, :], c == 0, c == PATCH - 1)
            last.then_inc(gram_ps, 1)

            def y_sums(f):
                pe.wait_ge(y_stats, IMG_R * (f + 1))
                mm(conv_ps[:, 0, 0:3 * IMG_R], same_channel[:, :], sum_1[:, :, :].rearrange("p a m -> p (a m)"),
                   True, True).then_inc(y_stats_ps, 1)

            def conv(f, m):
                n = IMG_R * f + m
                hold(pe, x_normed, n + 1)
                hold(pe, w_mid_ready, f + 1)
                for b in range(2):
                    if not (isinstance(f, int) and f == 0 and m == 0):
                        hold(pe, x1_done, 2 * n - 1 + b)
                    for i, kx in enumerate((0, 2, 1)):
                        wk = w_mid[:, m, :] if kx == 1 else w_taps[:, kx, :]
                        rows_ = slice(b * GR // 2, (b + 1) * GR // 2)
                        for half, src in enumerate((xa[:, m], xb[:, m % 2])):
                            part = slice(half * P // 2, (half + 1) * P // 2)
                            last = mm(conv_ps[part, b, :], wk[:, part], src[:, rows_, kx:kx + W], i == 0, i == 2, True)
                    last.then_inc(conv_done, 1)

            def correlate(f, s):
                pe.wait_ge(z_done, IMG_R * f + 2 * s + 2)
                if not (isinstance(f, int) and f == 0):
                    pe.wait_ge(h_read[s], STEPS * f)
                for t in range(TILES):
                    zt = z[:, 2 * s + t // 2, t % 2 * HALF:(t % 2 + 1) * HALF].rearrange("p (n c) -> p c n", c=PATCH)
                    for c in range(PATCH):
                        last = mm(h[s][:, t, :], zt[:, c, :], d_sb[:, c, :], t % 2 == 0 and c == 0, c == PATCH - 1, True)
                    if t % 2:
                        last.then_inc(h_ready[s], 1)

            def update(r, s, k):
                pe.wait_ge(rows_in[s][k], 16 * TILES * (r + 1))
                for t in range(TILES):
                    pe.wait_ge(diag_ready[s], TILES * (r * (STEPS - 1) + k) + t + 1)
                    for j in range(k + 1):
                        last = mm(h[s][:, t, :], diag[s][:, t, j, :], rows[s][:, j, t, :], False, j == k, True)
                    if t % 2:
                        last.then_inc(h_ready[s], 1)

            def coef_transposes(r, m):
                n = IMG_R * r + m
                pe.wait_ge(coef_ready, 2 * n + 2)
                pe.wait_ge(y_done, 2 * n + 2)
                for k in range(CHUNKS):
                    for t in range(2):
                        last = nc.tensor.transpose(back_ps[0][:, k, t * P:(t + 1) * P],
                                                   picked[:, m % 2, t, 0, k * P:(k + 1) * P], ident[:, :])
                last.then_inc(coef_t_ps, 1)

            def reconstruct(r, m):
                n = IMG_R * r + m
                pe.wait_ge(coef_t_done, n + 1)
                for half in (1, 0):
                    for c2 in range(2):
                        c = 2 * half + c2
                        if isinstance(n, int):
                            res = x1[:, n, c:PIX:PATCH]
                        else:
                            res = x1[:, bass.ds(n, 1), c:PIX:PATCH].rearrange("p a n -> p (a n)")
                        mm(back_ps[half][:, c2, :], ident[:, :], res, c2 == 0, False, True)
                        for k in range(CHUNKS):
                            last = mm(back_ps[half][:, c2, :], d_t[:, k, c, :], coef_t[:, k, :], False,
                                      k == CHUNKS - 1, True)
                    last.then_inc(recon_ps, 1)

            for m in range(IMG_R):
                conv(0, m)
            y_sums(0)
            pe.wait_ge(gram_sb_done, 1)
            pe.wait_ge(d_t_done, 1)
            correlate(0, 0)

            def body(r, front, behind):
                f = r + 1
                b = r - 1
                correlate(r, 1)
                if front:
                    x_sums(f)
                if behind:
                    coef_transposes(b, 0)
                    reconstruct(b, 0)
                update(r, 0, 0)
                if behind:
                    coef_transposes(b, 1)
                update(r, 1, 0)
                if front:
                    conv(f, 0)
                update(r, 0, 1)
                if front:
                    conv(f, 1)
                update(r, 1, 1)
                if front:
                    conv(f, 2)
                if behind:
                    reconstruct(b, 1)
                update(r, 0, 2)
                if front:
                    conv(f, 3)
                update(r, 1, 2)
                if front:
                    y_sums(f)
                update(r, 0, 3)
                if behind:
                    coef_transposes(b, 2)
                    reconstruct(b, 2)
                update(r, 1, 3)
                if behind:
                    coef_transposes(b, 3)
                    reconstruct(b, 3)
                if front:
                    correlate(f, 0)

            body(0, True, False)
            with pe.Fori(1, ROUNDS - 1) as r:
                body(r, True, True)
            body(ROUNDS - 1, False, True)
            for m in range(IMG_R):
                coef_transposes(ROUNDS - 1, m)
                reconstruct(ROUNDS - 1, m)

        @block.scalar
        def _(act):
            act.wait_ge(w_loaded, 16 * (4 * PATCH + 1))
            nc.scalar.activation(gate[:, 1:2], gate[:, 0:1], ACT.Sigmoid).then_inc(gate_done, 1)
            def x_statistics(f, m):
                hold(act, xa_loaded[m], 16 * PATCH * (f + 1))
                for i, func in enumerate((ACT.Copy, ACT.Square)):
                    n = 2 * m + i
                    if n >= 3:
                        hold(act, x_stats, 2 * IMG_R * f + n - 2)
                    nc.scalar.activation(unread[:, n % 3], xa[:, m, :, 1:W + 1], func,
                                         accum_out=sum_x[:, i, m:m + 1]).then_inc(x_stats, 1)

            def root(ready, done, which, f):
                act.wait_ge(ready, f + 1)
                nc.scalar.activation(gn[:, which, 5, :], gn[:, which, 4, :], ACT.Sqrt).then_inc(done, 1)

            def norm_x(f, m):
                if m == 0:
                    act.wait_ge(x_params, f + 1)
                act.wait_ge(xb_loaded[m % 2], 16 * PATCH * (2 * f + m // 2 + 1))
                bias, scale = gn[:, 0, 9, m:m + 1], gn[:, 0, 8, m:m + 1]
                inner = slice(0, (PATCH - 1) * C)
                for part in (xa[:, m, 1:GR], xa[inner, m, 0:1], xb[:, m % 2, 0:GR - 1], xb[inner, m % 2, GR - 1:GR]):
                    n_part = part.shape[0]
                    last = nc.scalar.activation(part[:, :, 1:W + 1], part[:, :, 1:W + 1], ACT.Identity,
                                                bias=bias[0:n_part], scale=scale[0:n_part])
                last.then_inc(x_normed, 1)

            def image_of(t, n):
                return t[:, n, :] if isinstance(n, int) else t[:, bass.ds(n, 1), :].rearrange("p a n -> p (a n)")

            def out_conv(f, m):
                n = IMG_R * f + m
                hold(act, conv_done, 2 * n + 2)
                for b in range(2):
                    nc.scalar.activation(image_of(x1, n)[:, b * HALF:(b + 1) * HALF], conv_ps[:, b, :], ACT.Identity,
                                         bias=gn[:, 0, 10, m:m + 1], accum_out=sum_1[:, b, m:m + 1]).then_inc(x1_done, 1)
                hold(act, x1_done, 2 * n + 2)
                nc.scalar.activation(z[:, m, :], image_of(x1, n), ACT.Square, accum_out=sum_1[:, 2, m:m + 1]
                                     ).then_inc(y_stats, 1)

            def norm_y(f, m):
                n = IMG_R * f + m
                if m == 0:
                    hold(act, y_params, f + 1)
                nc.scalar.activation(z[:, m, :], image_of(x1, n), ACT.Identity,
                                     bias=gn[:, 1, 9, m:m + 1], scale=gn[:, 1, 8, m:m + 1]).then_inc(z_done, 1)

            def scores(r, s, k):
                for b in range(2):
                    act.wait_ge(h_ready[s], 2 * (STEPS * r + k) + b + 1)
                    if b == 0 and not (isinstance(r, int) and r == 0 and k == 0):
                        act.wait_ge(h_read[s], STEPS * r + k)
                    nc.scalar.activation(score[s][:, 2 * b:2 * b + 2, :], h[s][:, 2 * b:2 * b + 2, :], ACT.Abs
                                         ).then_inc(score_ready[s], 1)

            def diags(r, s, k):
                act.wait_ge(dx_ready[s], (STEPS - 1) * r + k + 1)
                if not (isinstance(r, int) and r == 0 and k == 0):
                    act.wait_ge(h_ready[s], 2 * (STEPS * r + k) + 2)
                for t in range(TILES):
                    for j in range(k + 1):
                        last = nc.scalar.activation(diag[s][:, t, j, :], ident[:, :], ACT.Copy, scale=dx[s][:, t, j:j + 1])
                    last.then_inc(diag_ready[s], 1)

            def copy_coef(r, m):
                n = IMG_R * r + m
                act.wait_ge(coef_t_ps, n + 3)
                nc.scalar.activation(coef_t[:, :, :], back_ps[0][:, :, :], ACT.Copy, scale=-1.0).then_inc(coef_t_done, 1)

            def out_back(r, m):
                n = IMG_R * r + m
                dst = image_of(x1, n).rearrange("p (n c) -> p c n", c=PATCH)
                for q, half in enumerate((1, 0)):
                    hold(act, recon_ps, 2 * n + q + 1)
                    nc.scalar.activation(dst[:, 2 * half:2 * half + 2, :], back_ps[half][:, :, :], ACT.Copy).then_inc(y_done, 1)

            act.sem_inc(y_done, 2)
            x_statistics(0, 0)
            x_statistics(0, 1)
            act.wait_ge(d_loaded, 16 * PATCH)
            nc.scalar.activation(d_tmp[:, :, :], d_sb[:, :, :], ACT.Square).then_inc(d_sq, 1)
            x_statistics(0, 2)
            x_statistics(0, 3)
            act.wait_ge(d_nrm, 1)
            nc.scalar.activation(d_norm[:, 1, :], d_norm[:, 0, :], ACT.Sqrt).then_inc(d_root, 1)
            root(x_var, x_root, 0, 0)
            act.wait_ge(d_t_ps, 1)
            for k in range(CHUNKS):
                last = nc.scalar.activation(d_t[:, k, :, :].rearrange("p c n -> p (c n)"),
                                            back_ps[k][:, :, :].rearrange("p a n -> p (a n)"), ACT.Copy)
            last.then_inc(d_t_done, 1)
            norm_x(0, 0)
            norm_x(0, 1)
            for m in range(IMG_R):
                out_conv(0, m)
                if m + 2 < IMG_R:
                    norm_x(0, m + 2)
            root(y_var, y_root, 1, 0)
            for m in range(IMG_R):
                norm_y(0, m)
            scores(0, 0, 0)

            def body(r, front, behind):
                f = r + 1
                b = r - 1
                if front:
                    for m in range(IMG_R):
                        x_statistics(f, m)
                scores(r, 1, 0)
                if front:
                    root(x_var, x_root, 0, f)
                if behind:
                    copy_coef(b, 0)
                if front:
                    norm_x(f, 0)
                if behind:
                    out_back(b, 0)
                diags(r, 0, 0)
                scores(r, 0, 1)
                if behind:
                    copy_coef(b, 1)
                if front:
                    norm_x(f, 1)
                diags(r, 1, 0)
                scores(r, 1, 1)
                diags(r, 0, 1)
                if front:
                    out_conv(f, 0)
                scores(r, 0, 2)
                if front:
                    norm_x(f, 2)
                diags(r, 1, 1)
                if front:
                    out_conv(f, 1)
                scores(r, 1, 2)
                if front:
                    norm_x(f, 3)
                diags(r, 0, 2)
                if behind:
                    out_back(b, 1)
                if front:
                    out_conv(f, 2)
                scores(r, 0, 3)
                diags(r, 1, 2)
                if front:
                    out_conv(f, 3)
                scores(r, 1, 3)
                if front:
                    root(y_var, y_root, 1, f)
                diags(r, 0, 3)
                scores(r, 0, 4)
                if behind:
                    copy_coef(b, 2)
                if front:
                    norm_y(f, 0)
                    norm_y(f, 1)
                diags(r, 1, 3)
                if behind:
                    out_back(b, 2)
                scores(r, 1, 4)
                if behind:
                    copy_coef(b, 3)
                if front:
                    norm_y(f, 2)
                    norm_y(f, 3)
                if behind:
                    out_back(b, 3)
                if front:
                    scores(f, 0, 0)

            body(0, True, False)
            with act.Fori(1, ROUNDS - 1) as r:
                body(r, True, True)
            body(ROUNDS - 1, False, True)
            for m in range(IMG_R):
                copy_coef(ROUNDS - 1, m)
                out_back(ROUNDS - 1, m)

        @block.vector
        def _(dve):
            v = nc.vector
            n = 0

            def step(ins):
                nonlocal n
                n += 1
                ins.then_inc(dve_step, 1)
                return n

            def after(count):
                dve.wait_ge(dve_step, count)

            def sync():
                after(n)

            def restart():
                nonlocal n
                sync()
                dve.sem_clear(dve_step)
                n = 0

            for t in (xa, xb):
                step(v.memset(t[:, :, :, 0:1], 0.0))
                step(v.memset(t[:, :, :, W + 1:W + 2], 0.0))
            sync()
            for m in range(IMG_R):
                step(v.memset(xa[3 * C:4 * C, m, 0, :], 0.0))
                step(v.memset(xa[:, m, GR, :], 0.0))
            for m in range(2):
                step(v.memset(xb[3 * C:4 * C, m, GR - 1, :], 0.0))
            sync()
            dve.sem_inc(pads_zero, 1)
            for c in range(8):
                step(v.memset(rank[:, c:c + 1], 1024.0 * (8 - c)))
            for s in range(2):
                step(v.memset(n_inv[s][:, :, :, :], 0.0))
                step(v.memset(rd[s][:, :, :], 1.0))
            sync()
            for s in range(2):
                for k in range(STEPS):
                    step(v.memset(n_inv[s][:, :, k, k:k + 1], 1.0))
            step(v.memset(w_taps[:, :, :], 0.0))

            def variance(f, which, sums, done):
                g = gn[:, which]
                dve.wait_ge(sums, f + 1)
                first = 1 - which
                c = step(v.tensor_scalar(g[:, first:3, :].rearrange("p a m -> p (a m)"),
                                         conv_ps[:, 0, 0:(3 - first) * IMG_R], 1.0 / (H * W), None, ALU.mult))
                if which:
                    after(c)
                    c = step(v.tensor_tensor(g[:, 1, :], g[:, 0, :], g[:, 1, :], ALU.add))
                after(c)
                c = step(v.tensor_tensor(g[:, 3, :], g[:, 1, :], g[:, 1, :], ALU.mult))
                after(c)
                c = step(v.tensor_tensor(g[:, 3, :], g[:, 2, :], g[:, 3, :], ALU.subtract))
                after(c)
                v.tensor_scalar(g[:, 4, :], g[:, 3, :], 0.0, GN_EPS, ALU.max, ALU.add).then_inc(done, 1)

            def norm_params(f, which, root_done, done):
                g = gn[:, which]
                dve.wait_ge(root_done, f + 1)
                step(v.reciprocal(g[:, 6, :], g[:, 5, :]))
                sync()
                step(v.tensor_tensor(g[:, 6, :], g[:, 6, :], g[:, 4, :], ALU.mult))
                sync()
                step(v.tensor_tensor(g[:, 7, :], g[:, 5, :], g[:, 6, :], ALU.add))
                sync()
                step(v.tensor_scalar(g[:, 7, :], g[:, 7, :], 0.5, None, ALU.mult))
                sync()
                step(v.reciprocal(g[:, 8, :], g[:, 7, :]))
                step(v.tensor_scalar(g[:, 10, :], g[:, 1, :], b_eff[:, 0:1], None, ALU.add))
                sync()
                v.scalar_tensor_tensor(out=g[:, 9, :], in0=g[:, 1, :], scalar=-1.0, in1=g[:, 8, :],
                                       op0=ALU.mult, op1=ALU.mult).then_inc(done, 1)

            def middle_weights(f):
                for m in range(IMG_R):
                    c = step(v.scalar_tensor_tensor(out=w_mid[:, m, :], in0=center[:, :], scalar=gn[:, 0, 7, m:m + 1],
                                                    in1=w_taps[:, 1, :], op0=ALU.mult, op1=ALU.add))
                after(c)
                dve.sem_inc(w_mid_ready, 1)

            def scan(r, s, k, other=iter(())):
                first = []
                for t in range(TILES):
                    if t % 2 == 0:
                        hold(dve, score_ready[s], 2 * (STEPS * r + k) + t // 2 + 1)
                    first.append(step(v.max(out=top[s][:, t, :], in_=score[s][:, t, :])))
                    next(other, None)
                for t in range(TILES):
                    after(first[t])
                    step(v.max_index(out=top_i[s][:, t, :], in_max=top[s][:, t, :], in_values=score[s][:, t, :]))
                    next(other, None)
                    next(other, None)
                for _ in other:
                    pass

            def select(r, s, k, other=iter(())):
                sync()
                if k == 0:
                    step(v.memset(x_neg[s][:, :, 1:STEPS], 0.0))
                    step(v.tensor_copy(idx_u[s][:, 0, :], top_i[s][:, :, 0]))
                    c = step(v.tensor_copy(idx[s][:, :, 0], top_i[s][:, :, 0]))
                else:
                    by_rank = rank[:, :].rearrange("p (a c) -> p a c", a=1).to_broadcast([P, TILES, 8])
                    if k == 1:
                        step(v.tensor_tensor(keep[s][:, :, :], top_i[s][:, :, :],
                                             idx[s][:, :, 0:1].to_broadcast([P, TILES, 8]), ALU.not_equal))
                        c = step(v.tensor_tensor(enc[s][:, :, :], top_i[s][:, :, :], by_rank, ALU.add))
                        next(other, None)
                    else:
                        i8 = top_i[s][:, :, :].rearrange("p t (c a) -> p t c a", a=1).to_broadcast([P, TILES, 8, k])
                        old = idx[s][:, :, 0:k].rearrange("p t (a j) -> p t a j", a=1).to_broadcast([P, TILES, 8, k])
                        c = step(v.tensor_tensor(free[s][:, :, :, 0:k], i8, old, ALU.not_equal))
                        step(v.tensor_tensor(enc[s][:, :, :], top_i[s][:, :, :], by_rank, ALU.add))
                        after(c)
                        c = step(v.tensor_reduce(keep[s][:, :, :], free[s][:, :, :, 0:k], AX.X, ALU.min))
                        next(other, None)
                    after(c)
                    c = step(v.tensor_tensor(enc[s][:, :, :], enc[s][:, :, :], keep[s][:, :, :], ALU.mult))
                    next(other, None)
                    after(c)
                    c = step(v.tensor_reduce(best[s][:, :], enc[s][:, :, :], AX.X, ALU.max))
                    next(other, None)
                    after(c)
                    c = step(v.tensor_scalar(idx_u[s][:, k, :], best[s][:, :], 1023, None, ALU.bitwise_and))
                    next(other, None)
                    after(c)
                    c = step(v.tensor_copy(idx[s][:, :, k], idx_u[s][:, k, :]))
                    next(other, None)
                after(c)
                if k < STEPS - 1:
                    dve.sem_inc(idx_ready[s], 1)
                else:
                    step(v.tensor_copy(idx_last[s][:, :, :], idx[s][:, :, :]))

            junk_n = [0]

            def pick(s, t, k, source, dst):
                if junk_n[0] >= JUNK:
                    after(junk_c[junk_n[0] % JUNK])
                junk_c[junk_n[0] % JUNK] = step(v.scalar_tensor_tensor(
                    out=junk[:, junk_n[0] % JUNK, :], in0=iota[:, :], scalar=idx[s][:, t, k:k + 1],
                    in1=source, op0=ALU.is_equal, op1=ALU.mult, accum_out=dst))
                junk_n[0] += 1

            junk_c = [0] * JUNK

            def extract(r, s, k, other=iter(())):
                for j in range(k):
                    if j == k - 1:
                        dve.wait_ge(rows_in[s][j], 16 * TILES * (r + 1))
                    for t in range(TILES):
                        pick(s, t, k, rows[s][:, j, t, :], g_at[s][:, t, j:j + 1])
                        next(other, None)
                for t in range(TILES):
                    pick(s, t, k, h[s][:, t, :], h_at[s][:, t:t + 1])
                    next(other, None)
                for _ in other:
                    pass

            def solve(r, s, k):
                T = TILES
                sync()
                dve.sem_inc(h_read[s], 1)
                if k > 0:
                    g_b = g_at[s][:, :, 0:k].rearrange("p t (a j) -> p t a j", a=1).to_broadcast([P, T, k, k])
                    c = step(v.tensor_tensor(prod[s][:, :, 0:k, 0:k], n_inv[s][:, :, 0:k, 0:k], g_b, ALU.mult))
                    yield
                    after(c)
                    c = step(v.tensor_reduce(w_vec[s][:, :, 0:k], prod[s][:, :, 0:k, 0:k], AX.X, ALU.add))
                    yield
                    after(c)
                    c = step(v.tensor_tensor(a_vec[s][:, :, 0:k], w_vec[s][:, :, 0:k], rd[s][:, :, 0:k], ALU.mult))
                    yield
                    after(c)
                    c = step(v.tensor_tensor(aw[s][:, :, 0:k], a_vec[s][:, :, 0:k], w_vec[s][:, :, 0:k], ALU.mult))
                    a_b = a_vec[s][:, :, 0:k].rearrange("p t (a i) -> p t a i", a=1).to_broadcast([P, T, k, k])
                    c2 = step(v.tensor_tensor(prod[s][:, :, 0:k, 0:k],
                                              n_inv[s][:, :, 0:k, 0:k].rearrange("p t i j -> p t j i"), a_b, ALU.mult))
                    yield
                    after(c)
                    c = step(v.tensor_reduce(d_neg[s][:, :], aw[s][:, :, 0:k], AX.X, ALU.add, negate=True))
                    after(c2)
                    c2 = step(v.tensor_reduce(n_inv[s][:, :, k, 0:k], prod[s][:, :, 0:k, 0:k], AX.X, ALU.add, negate=True))
                    yield
                    after(c)
                    c = step(v.tensor_scalar(d_k[s][:, :], d_neg[s][:, :], 1.0, DIAG_EPS, ALU.add, ALU.max))
                    yield
                    after(c)
                    c = step(v.reciprocal(rd[s][:, :, k], d_k[s][:, :]))
                    yield
                    after(c)
                c = step(v.scalar_tensor_tensor(out=c_neg[s][:, :], in0=h_at[s][:, :], scalar=-1.0, in1=rd[s][:, :, k],
                                                op0=ALU.mult, op1=ALU.mult))
                yield
                after(c)
                c_b = c_neg[s][:, :].rearrange("p (t a) -> p t a", a=1).to_broadcast([P, T, k + 1])
                c = step(v.tensor_tensor(dx[s][:, :, 0:k + 1], n_inv[s][:, :, k, 0:k + 1], c_b, ALU.mult))
                yield
                after(c)
                if k < STEPS - 1:
                    dve.sem_inc(dx_ready[s], 1)
                if k == 0:
                    step(v.tensor_copy(x_neg[s][:, :, 0], dx[s][:, :, 0]))
                else:
                    total = x_neg[s] if k < STEPS - 1 else x_last[s]
                    step(v.tensor_tensor(total[:, :, 0:k + 1], x_neg[s][:, :, 0:k + 1], dx[s][:, :, 0:k + 1], ALU.add))

            def scatter(r, m):
                hold(dve, coef_t_ps, IMG_R * r + m + 1)
                for t in range(2):
                    tile = 2 * (m % 2) + t
                    for j in range(STEPS):
                        c = step(v.tensor_scalar(picked[:, m % 2, t, j, :], iota[:, :], idx_last[m // 2][:, tile, j:j + 1],
                                                 x_last[m // 2][:, tile, j:j + 1], ALU.is_equal, ALU.mult))
                        yield
                    after(c)
                    dve.sem_inc(picked_ready, 1)

            def together(*parts):
                parts = list(parts)
                while parts:
                    parts = [p for p in parts if next(p, parts) is not parts]

            dve.wait_ge(w_loaded, 16 * (4 * PATCH + 1))
            step(v.tensor_reduce(w_sum[:, :], w_raw[:, :, :], AX.X, ALU.add, apply_absolute_value=True))
            sync()
            dve.sem_inc(w_sum_ready, 1)
            dve.wait_ge(w_sum_ps, 1)
            step(v.tensor_scalar(w_scale[:, 0:2], conv_ps[:, 0, 0:2], 1.0 / (PATCH * C * C * TAPS), SCALE_EPS, ALU.mult, ALU.max))
            sync()
            step(v.tensor_scalar(w_scale[:, 2:4], w_scale[:, 0:2], 0.5, None, ALU.mult))
            dve.wait_ge(gate_done, 1)
            sync()
            for i in range(2):
                step(v.tensor_scalar(w_tmp[:, 0, :], w_raw[:, i, :], w_scale[:, 2 + i:3 + i], w_scale[:, i:i + 1], ALU.is_gt, ALU.mult))
                step(v.tensor_scalar(w_tmp[:, 1, :], w_raw[:, i, :], -1.0, w_scale[:, 2 + i:3 + i], ALU.mult, ALU.is_gt))
                sync()
                step(v.tensor_scalar(w_tmp[:, 1, :], w_tmp[:, 1, :], w_scale[:, i:i + 1], None, ALU.mult))
                sync()
                step(v.tensor_tensor(w_raw[:, i, :], w_tmp[:, 0, :], w_tmp[:, 1, :], ALU.subtract))
                sync()
            step(v.scalar_tensor_tensor(out=w_tmp[:, 2, :], in0=w_raw[:, 1, :], scalar=gate[:, 1:2], in1=w_raw[:, 0, :],
                                        op0=ALU.mult, op1=ALU.add))
            step(v.scalar_tensor_tensor(out=b_eff[:, :], in0=b_raw[:, 1:2], scalar=gate[:, 1:2], in1=b_raw[:, 0:1],
                                        op0=ALU.mult, op1=ALU.add))
            sync()
            for tap in range(TAPS):
                step(v.transpose(w_t[:, tap, :], w_tmp[:, 2, :].rearrange("p (i t) -> p t i", t=TAPS)[:, tap, :]))
            sync()
            for p in range(PATCH):
                held_rows = (0, 1, 2, -1) if p < 2 else (1, 2, 3, 4)
                for q in range(PATCH):
                    ky = held_rows[q] - p + 1
                    if 0 <= ky < 3:
                        part = slice(q * C, (q + 1) * C)
                        step(v.tensor_copy(w_taps[part, :, p * C:(p + 1) * C], w_t[part, 3 * ky:3 * ky + 3, :]))
            sync()
            dve.sem_inc(w_ready, 1)
            dve.wait_ge(const_done, 1)
            variance(0, 0, x_stats_ps, x_var)
            dve.wait_ge(d_sq_ps, 1)
            step(v.tensor_copy(d_norm[:, 0, :], conv_ps[:, 1, 0:ATOMS]))
            sync()
            dve.sem_inc(d_nrm, 1)
            norm_params(0, 0, x_root, x_params)
            dve.wait_ge(d_root, 1)
            step(v.reciprocal(d_norm[:, 2, :], d_norm[:, 1, :]))
            sync()
            step(v.tensor_tensor(d_norm[:, 3, :], d_norm[:, 2, :], d_norm[:, 0, :], ALU.mult))
            sync()
            step(v.tensor_tensor(d_norm[:, 2, :], d_norm[:, 3, :], d_norm[:, 1, :], ALU.add))
            sync()
            step(v.tensor_scalar(d_norm[:, 3, :], d_norm[:, 2, :], 0.5, NORM_EPS, ALU.mult, ALU.add))
            sync()
            step(v.reciprocal(d_norm[:, 2, :], d_norm[:, 3, :]))
            sync()
            for c in range(PATCH):
                step(v.tensor_tensor(d_sb[:, c, :], d_sb[:, c, :], d_norm[:, 2, :], ALU.mult))
            sync()
            dve.sem_inc(d_ready, 1)
            middle_weights(0)
            dve.wait_ge(gram_ps, 1)
            for k in range(CHUNKS):
                step(v.tensor_copy(gram[:, k, :], h[0][:, 2 * k, :]))
            sync()
            for k in range(CHUNKS):
                step(v.scalar_tensor_tensor(out=gram[:, k, k * P:(k + 1) * P], in0=ident[:, :], scalar=DIAG_EPS,
                                            in1=gram[:, k, k * P:(k + 1) * P], op0=ALU.mult, op1=ALU.add))
            sync()
            dve.sem_inc(gram_sb_done, 1)
            variance(0, 1, y_stats_ps, y_var)
            norm_params(0, 1, y_root, y_params)

            def body(r, front, behind):
                f = r + 1
                restart()
                junk_n[0] = 0
                nothing = iter(())
                for k in range(STEPS):
                    rows_of = scatter(r - 1, k + 1) if behind and k in (1, 2) else nothing
                    scan(r, 0, k, solve(r, 1, k - 1) if k else nothing)
                    select(r, 0, k, rows_of)
                    if front and k == 0:
                        variance(f, 0, x_stats_ps, x_var)
                    extract(r, 0, k)
                    if front and k == 0:
                        norm_params(f, 0, x_root, x_params)
                        middle_weights(f)
                    if front and k == 3:
                        variance(f, 1, y_stats_ps, y_var)
                    scan(r, 1, k, solve(r, 0, k))
                    if k == STEPS - 1:
                        rows_of = scatter(r, 0)
                    select(r, 1, k, rows_of)
                    if k < STEPS - 1:
                        together(rows_of)
                    if front and k == 3:
                        norm_params(f, 1, y_root, y_params)
                    extract(r, 1, k)
                together(solve(r, 1, STEPS - 1), rows_of)
                together(scatter(r, 1))

            body(0, True, False)
            with dve.Fori(1, ROUNDS - 1) as r:
                body(r, True, True)
            body(ROUNDS - 1, False, True)
            for m in range(2, IMG_R):
                together(scatter(ROUNDS - 1, m))


_INS = ['x', 'L0_conv_w', 'L0_conv_b', 'L0_conv_w_child', 'L0_conv_b_child', 'L0_conv_gate', 'L1_conv_dictionary']


def kernel(**inputs):
    import numpy as _np
    import concourse.bacc as _bacc
    from concourse import mybir as _mybir
    from concourse.bass_utils import run_bass_kernel_spmd as _run

    nc = _bacc.Bacc("TRN2", target_bir_lowering=False, num_devices=1)
    arrays, args = {}, []
    for name in _INS:
        a = _np.ascontiguousarray(inputs[name])
        arrays[f"in_{name}"] = a
        args.append(nc.dram_tensor(f"in_{name}", a.shape, _mybir.dt.from_np(a.dtype), kind="ExternalInput").ap())
    result = nc.dram_tensor("out_0", inputs['x'].shape, _mybir.dt.float32, kind="ExternalOutput").ap()
    build_program(nc, *args, result)
    r = _run(nc, [arrays], core_ids=[0])
    return r.results[0]["out_0"]
```

```python
import numpy as np
import concourse.bass as bass
import concourse.mybir as mybir
from contextlib import ExitStack

F32 = mybir.dt.float32
BF16 = mybir.dt.bfloat16
U32 = mybir.dt.uint32
ALU = mybir.AluOpType
ACT = mybir.ActivationFunctionType
AX = mybir.AxisListType


def build_program(nc, x_in, w_in, b_in, wc_in, bc_in, gate_in, dict_in, out):
    IMAGES, C, H, W = x_in.shape
    P = 128
    ATOM_DIM, ATOMS = dict_in.shape
    PATCH = 4
    GR = H // PATCH
    PIX = GR * W
    PAD_W = W + 2
    STEPS = 5
    IMG_R = 4
    ROUNDS = IMAGES // IMG_R
    TILES = 4
    CHUNKS = ATOMS // P
    TAPS = 9
    HALF = PIX // 2
    GN_EPS = 1e-5
    DIAG_EPS = 1e-5
    SCALE_EPS = 1e-5
    NORM_EPS = 1e-10
    JUNK = 3
    DVE_SQUARES = (1, 3)
    MASKED = 3

    ctx = ExitStack()
    with ctx:
        def sb(name, shape, dt=F32):
            return ctx.enter_context(nc.sbuf_tensor(name, shape, dt))

        def sem(name):
            return ctx.enter_context(nc.semaphore(name))

        gram_dram = nc.dram_tensor("gram", [ATOMS, ATOMS], F32, kind="Internal").ap()

        ident = sb("ident", [P, P])
        same_channel = sb("same_channel", [P, P])
        center = sb("center", [P, P])
        iota = sb("iota", [P, ATOMS])
        iota_short = sb("iota_short", [P, ATOMS], BF16)
        rank = sb("rank", [P, 8])
        w_taps = sb("w_taps", [P, 3, P])
        w_mid = sb("w_mid", [P, IMG_R, P])
        w_sum = sb("w_sum", [P, 2])
        w_scale = sb("w_scale", [P, 4])
        gate = sb("gate", [P, 3])
        b_raw = sb("b_raw", [P, 2])
        b_eff = sb("b_eff", [P, 1])
        d_sb = sb("d_sb", [P, PATCH, ATOMS])
        d_t = sb("d_t", [P, CHUNKS, PATCH, P])
        xa = sb("xa", [P, IMG_R, GR + 1, PAD_W])
        sum_x = sb("sum_x", [P, 2, IMG_R])
        sum_1 = sb("sum_1", [P, 3, IMG_R])
        gn = sb("gn", [P, 2, 12, IMG_R])
        xb = sb("xb", [P, 2, GR, PAD_W])
        x1 = sb("x1", [P, IMAGES, PIX])
        z = sb("z", [P, IMG_R, PIX])
        score = [sb(f"score{s}", [P, TILES, ATOMS]) for s in range(2)]
        rows = [sb(f"rows{s}", [P, STEPS - 1, TILES, ATOMS]) for s in range(2)]
        diag = [sb(f"diag{s}", [P, TILES, STEPS - 1, P]) for s in range(2)]
        junk = sb("junk", [P, JUNK, ATOMS], BF16)
        mask = sb("mask", [P, TILES, ATOMS], BF16)
        top = [sb(f"top{s}", [P, TILES, 8]) for s in range(2)]
        top_i = [sb(f"top_i{s}", [P, TILES, 8], U32) for s in range(2)]
        enc = [sb(f"enc{s}", [P, TILES, 8]) for s in range(2)]
        free = [sb(f"free{s}", [P, TILES, 8, STEPS - 1]) for s in range(2)]
        keep = [sb(f"keep{s}", [P, TILES, 8]) for s in range(2)]
        best = [sb(f"best{s}", [P, TILES], U32) for s in range(2)]
        idx_u = [sb(f"idx_u{s}", [P, STEPS, TILES], U32) for s in range(2)]
        h_at = [sb(f"h_at{s}", [P, TILES]) for s in range(2)]
        g_at = [sb(f"g_at{s}", [P, TILES, STEPS - 1]) for s in range(2)]
        n_inv = [sb(f"n_inv{s}", [P, TILES, STEPS, STEPS]) for s in range(2)]
        prod = [sb(f"prod{s}", [P, TILES, STEPS - 1, STEPS - 1]) for s in range(2)]
        w_vec = [sb(f"w_vec{s}", [P, TILES, STEPS - 1]) for s in range(2)]
        a_vec = [sb(f"a_vec{s}", [P, TILES, STEPS - 1]) for s in range(2)]
        aw = [sb(f"aw{s}", [P, TILES, STEPS - 1]) for s in range(2)]
        d_neg = [sb(f"d_neg{s}", [P, TILES]) for s in range(2)]
        d_k = [sb(f"d_k{s}", [P, TILES]) for s in range(2)]
        rd = [sb(f"rd{s}", [P, TILES, STEPS]) for s in range(2)]
        c_neg = [sb(f"c_neg{s}", [P, TILES]) for s in range(2)]
        dx = [sb(f"dx{s}", [P, TILES, STEPS]) for s in range(2)]
        x_neg = [sb(f"x_neg{s}", [P, TILES, STEPS]) for s in range(2)]
        x_last = [sb(f"x_last{s}", [P, TILES, STEPS]) for s in range(2)]
        idx_last = [sb(f"idx_last{s}", [P, TILES, STEPS]) for s in range(2)]
        picked = sb("picked", [P, 2, 2, STEPS, ATOMS])
        coef_t = sb("coef_t", [P, CHUNKS, 2 * P])
        spare = picked[:, :, :, :, :].rearrange("p a b j n -> p (a b) (j n)")
        w_raw = spare[:, 0, 0:2 * C * TAPS].rearrange("p (i n) -> p i n", i=2)
        w_tmp = spare[:, 1, 0:3 * C * TAPS].rearrange("p (i n) -> p i n", i=3)
        ones = diag[0][:, 0, 0, :]
        xb_first = rows[0][:, :, :, :].rearrange("p j t n -> p (j t n)")[:, 0:2 * GR * PAD_W].rearrange(
            "p (m g w) -> p m g w", m=2, w=PAD_W)
        d_tmp = x1[:, IMAGES - 1, :].rearrange("p (c a) -> p c a", a=ATOMS)
        d_norm = x1[:, IMAGES - 2, :].rearrange("p (c a) -> p c a", a=ATOMS)
        w_t = spare[:, 2, 0:TAPS * C].rearrange("p (t c) -> p t c", c=C)
        gram = coef_t[:, :, :]
        def three_images(t):
            return t.bitcast(BF16)[:, 0:3 * (GR + 1) * W].rearrange("p (a g w) -> p a g w", a=3, w=W)

        unread = three_images(z[:, 0:2, :].rearrange("p m n -> p (m n)"))
        unread_first = three_images(diag[1][:, :, :, :].rearrange("p t j n -> p (t j n)"))
        iota_i = junk[:, 0:2, :].rearrange("p a n -> p (a n)").bitcast(U32)

        h = [ctx.enter_context(nc.psum_tensor(f"h{s}", [P, TILES, ATOMS], F32)) for s in range(2)]
        conv_ps = ctx.enter_context(nc.psum_tensor("conv_ps", [P, 2, HALF], F32))
        back_ps = [ctx.enter_context(nc.psum_tensor(f"back_ps{b}", [P, 2, 2 * P], F32)) for b in range(2)]

        final_ps = conv_ps[:, 0, :].rearrange("p (k n) -> p k n", k=CHUNKS)

        const_done = sem("const_done")
        gate_loaded = sem("gate_loaded")
        w_loaded = sem("w_loaded")
        d_loaded = sem("d_loaded")
        pads_zero = sem("pads_zero")
        w_sum_ready = sem("w_sum_ready")
        w_sum_ps = sem("w_sum_ps")
        gate_done = sem("gate_done")
        w_ready = sem("w_ready")
        d_sq = sem("d_sq")
        d_sq_ps = sem("d_sq_ps")
        d_nrm = sem("d_nrm")
        d_root = sem("d_root")
        d_ready = sem("d_ready")
        d_t_ps = sem("d_t_ps")
        d_t_done = sem("d_t_done")
        gram_ps = sem("gram_ps")
        gram_sb_done = sem("gram_sb_done")
        gram_stored = sem("gram_stored")
        xa_loaded = [sem(f"xa_loaded{m}") for m in range(IMG_R)]
        xb_loaded = [sem(f"xb_loaded{m}") for m in range(2)]
        xb_first_loaded = [sem(f"xb_first_loaded{m}") for m in range(2)]
        x_stats = sem("x_stats")
        x_stats_ps = sem("x_stats_ps")
        x_var = sem("x_var")
        x_root = sem("x_root")
        x_params = sem("x_params")
        x_normed = sem("x_normed")
        x_normed_act = sem("x_normed_act")
        w_mid_ready = sem("w_mid_ready")
        conv_done = sem("conv_done")
        x1_done = sem("x1_done")
        y_stats = sem("y_stats")
        y_stats_ps = sem("y_stats_ps")
        y_var = sem("y_var")
        y_root = sem("y_root")
        y_params = sem("y_params")
        z_done = sem("z_done")
        h_ready = [sem(f"h_ready{s}") for s in range(2)]
        score_ready = [sem(f"score_ready{s}") for s in range(2)]
        idx_ready = [sem(f"idx_ready{s}") for s in range(2)]
        rows_in = [[sem(f"rows_in{s}_{j}") for j in range(STEPS - 1)] for s in range(2)]
        dx_ready = [sem(f"dx_ready{s}") for s in range(2)]
        diag_ready = [sem(f"diag_ready{s}") for s in range(2)]
        h_read = [sem(f"h_read{s}") for s in range(2)]
        picked_ready = sem("picked_ready")
        coef_ready = sem("coef_ready")
        coef_ready_dve = sem("coef_ready_dve")
        coef_t_ps = sem("coef_t_ps")
        coef_t_done = sem("coef_t_done")
        recon_ps = sem("recon_ps")
        y_done = sem("y_done")
        y_stored = sem("y_stored")
        dve_step = sem("dve_step")
        pool_step = sem("pool_step")

        block = ctx.enter_context(nc.Block())

        held = {eng: sem(f"held_{name}") for name, eng in (('pool', nc.gpsimd), ('pe', nc.tensor), ('act', nc.scalar), ('dve', nc.vector))}

        def b_part(f, m):
            return xb_first[:, m - 2] if isinstance(f, int) and f == 0 and m >= 2 else xb[:, m % 2]

        def image_parts(f, m):
            b = b_part(f, m)
            inner = slice(0, (PATCH - 1) * C)
            return [part[:, :, 1:W + 1] for part in (xa[:, m, 1:GR], b[:, 0:GR - 1],
                                                     xa[inner, m, 0:1], b[inner, GR - 1:GR])]

        def hold(eng, signal, value):
            eng.wait_ge(signal, value)
            eng.sem_inc(held[eng], 1)

        @block.sync
        def _(sp):
            def rows_by_group(image):
                return image.rearrange("c (g q) w -> q c g w", q=PATCH)

            def source(n):
                return x_in[n] if isinstance(n, int) else x_in[bass.ds(n, 1)].rearrange("a c r w -> (a c) r w")

            first = slice(0, 3 * C)
            last = slice(3 * C, 4 * C)

            def load_a(n, m):
                src = source(n)
                sp.dma_start(xa[first, m, 0:GR, 1:W + 1],
                             rows_by_group(src)[0:3]).then_inc(xa_loaded[m], 16)
                sp.dma_start(xa[last, m, 1:GR + 1, 1:W + 1], src[:, PATCH - 1:H:PATCH, :]).then_inc(xa_loaded[m], 16)

            def load_b(n, part, loaded):
                src = source(n)
                sp.dma_start(part[first, 0:GR, 1:W + 1], rows_by_group(src)[1:4]).then_inc(loaded, 16)
                sp.dma_start(part[last, 0:GR - 1, 1:W + 1], src[:, PATCH:H:PATCH, :]).then_inc(loaded, 16)

            def for_all_groups(t):
                return t.rearrange("(a o) n -> a o n", a=1).to_broadcast([PATCH, C, t.shape[1]])

            sp.dma_start(gate[:, 0:1], gate_in.rearrange("(a b) -> a b", a=1).to_broadcast([P, 1])).then_inc(gate_loaded, 16)
            load_a(0, 0)
            for i, (w_d, b_d) in enumerate([(w_in, b_in), (wc_in, bc_in)]):
                sp.dma_start(w_raw[:, i, :],
                             for_all_groups(w_d.rearrange("o i a b -> o (i a b)"))).then_inc(w_loaded, 16)
                sp.dma_start(b_raw[:, i:i + 1],
                             for_all_groups(b_d.rearrange("(o i) -> o i", i=1))).then_inc(w_loaded, 16)
            load_a(1, 1)
            load_a(2, 2)
            load_a(3, 3)
            d_view = dict_in.rearrange("(c r x) a -> r c (x a)", r=PATCH, x=PATCH)
            for q in range(PATCH):
                sp.dma_start(d_sb[q * C:(q + 1) * C, :, :].rearrange("p x a -> p (x a)"), d_view[q]).then_inc(d_loaded, 16)
            for m in range(IMG_R):
                load_b(m, b_part(0, m), xb_loaded[m] if m < 2 else xb_first_loaded[m - 2])

            def loads_ahead(f, more=True):
                for m in range(IMG_R):
                    n = IMG_R * f + m
                    if more or m + 2 < IMG_R:
                        sp.wait_ge(conv_done, 2 * n + 2)
                    if isinstance(f, int) and f == 0:
                        if m < 2:
                            load_b(n + IMG_R, xb[:, m], xb_loaded[m])
                    elif more or m + 2 < IMG_R:
                        load_b(n + 2, xb[:, m % 2], xb_loaded[m % 2])
                    if more:
                        load_a(n + IMG_R, m)

            def store(r, m):
                n = IMG_R * r + m
                sp.wait_ge(y_done, 2 * n + 4)
                dst = out[n] if isinstance(n, int) else out[bass.ds(n, 1)].rearrange("a c r w -> (a c) r w")
                src = x1[:, n, :] if isinstance(n, int) else x1[:, bass.ds(n, 1), :].rearrange("p a n -> p (a n)")
                sp.dma_start(rows_by_group(dst), src.rearrange("p (g w) -> p g w", w=W)).then_inc(y_stored, 16)

            def body(r, front, more, behind):
                if behind:
                    store(r - 1, 0)
                if front:
                    loads_ahead(r + 1, more)
                if behind:
                    for m in range(1, IMG_R):
                        store(r - 1, m)

            loads_ahead(0)
            sp.wait_ge(gram_sb_done, 1)
            sp.dma_start(gram_dram.rearrange("(k p) a -> p k a", p=P), gram[:, :, :]).then_inc(gram_stored, 16)
            body(0, True, True, False)
            with sp.Fori(1, ROUNDS - 2) as r:
                body(r, True, True, True)
            body(ROUNDS - 2, True, False, True)
            body(ROUNDS - 1, False, False, True)
            for m in range(IMG_R):
                store(ROUNDS - 1, m)
            sp.wait_ge(y_stored, 16 * IMAGES)

        @block.gpsimd
        def _(pool):
            n = 0

            def step(ins):
                nonlocal n
                n += 1
                ins.then_inc(pool_step, 1)
                pool.wait_ge(pool_step, n)

            step(nc.gpsimd.memset(ident[:, :], 0.0))
            step(nc.gpsimd.memset(same_channel[:, :], 0.0))
            step(nc.gpsimd.memset(center[:, :], 0.0))
            step(nc.gpsimd.memset(ones, 1.0))
            step(nc.gpsimd.iota(iota_i[:, :], pattern=[[1, ATOMS]], base=0, channel_multiplier=0))

            def put_ones(t, offset):
                step(nc.gpsimd.affine_select(out=t, in_=t, compare_op=ALU.not_equal, fill=1.0,
                                             base=-offset, pattern=[[1, t.shape[1]]], channel_multiplier=-1))

            put_ones(ident[:, :], 0)
            for q in range(1 - PATCH, PATCH):
                put_ones(same_channel[:, :], q * C)
            put_ones(center[:, 0:P // 2], 0)
            put_ones(center[:, P // 2:P], -C)
            step(nc.gpsimd.tensor_copy(iota_short[:, :], iota_i[:, :]))
            nc.gpsimd.tensor_copy(iota[:, :], iota_i[:, :]).then_inc(const_done, 1)

            def gather(r, s, k):
                hold(pool, idx_ready[s], (STEPS - 1) * r + k + 1)
                for t in range(TILES):
                    pool.indirect_dma_start(out=rows[s][:, k, t, :], out_offset=None, in_=gram_dram[:, :],
                                            in_offset=bass.IndirectOffsetOnAxis(ap=idx_u[s][:, k, t:t + 1], axis=0)
                                            ).then_inc(rows_in[s][k], 16)

            pool.wait_ge(gram_stored, 16)

            pool_base = n

            def sum_picked(r, m, tiles=(0, 1), left_out=0):
                for t in tiles:
                    hold(pool, picked_ready, 2 * (IMG_R * r + m) + t + 1)
                    for j in range(1, STEPS):
                        last = nc.gpsimd.tensor_tensor(picked[:, m % 2, t, 0, :], picked[:, m % 2, t, 0, :],
                                                       picked[:, m % 2, t, j, :], ALU.add)
                        if j < STEPS - 1:
                            count = pool_base + 2 * (STEPS - 2) * (IMG_R * r + m) + (STEPS - 2) * (t - left_out) + j
                            last.then_inc(pool_step, 1)
                            hold(pool, pool_step, count)
                    last.then_inc(coef_ready, 1)

            def body(r, behind):
                for k in range(STEPS - 1):
                    for s in range(2):
                        gather(r, s, k)
                        if behind and (s, k) in sums_after:
                            sum_picked(r - 1, sums_after[s, k])
                sum_picked(r, 0)

            sums_after = {(1, 0): 1, (0, 2): 2, (0, 3): 3}
            body(0, False)
            with pool.Fori(1, ROUNDS) as r:
                body(r, True)
            sum_picked(ROUNDS - 1, 1)
            sum_picked(ROUNDS - 1, 2, (0,))
            sum_picked(ROUNDS - 1, 3, (0,), 1)

        @block.tensor
        def _(pe):
            def mm(dst, lhs, rhs, start, stop, skip=False):
                return nc.tensor.matmul(dst, lhs, rhs, start=start, stop=stop, skip_group_check=skip)

            pe.sem_inc(coef_t_ps, 2)
            pe.wait_ge(const_done, 1)
            pe.wait_ge(w_sum_ready, 1)
            mm(conv_ps[:, 0, 0:2], ones, w_sum[:, :], True, True).then_inc(w_sum_ps, 1)
            def x_sums(f):
                pe.wait_ge(x_stats, 2 * IMG_R * (f + 1))
                mm(conv_ps[:, 0, 0:2 * IMG_R], same_channel[:, :], sum_x[:, :, :].rearrange("p a m -> p (a m)"),
                   True, True).then_inc(x_stats_ps, 1)

            pe.wait_ge(w_ready, 1)
            x_sums(0)
            pe.wait_ge(d_sq, 1)
            for c in range(PATCH):
                last = mm(back_ps[0][:, 0, :], ones, d_tmp[:, c, :], c == 0, c == PATCH - 1)
            last.then_inc(d_sq_ps, 1)
            def transpose_atoms():
                pe.wait_ge(d_ready, 1)
                for k in range(CHUNKS):
                    for c in range(PATCH):
                        last = nc.tensor.transpose(back_ps[k][:, c // 2, c % 2 * P:(c % 2 + 1) * P],
                                                   d_sb[:, c, k * P:(k + 1) * P], ident[:, :])
                last.then_inc(d_t_ps, 1)

            def gram_matrix():
                for k in range(CHUNKS):
                    for c in range(PATCH):
                        last = mm(h[1][:, 2 * k, :], d_sb[:, c, k * P:(k + 1) * P], d_sb[:, c, :], c == 0, c == PATCH - 1)
                last.then_inc(gram_ps, 1)

            def y_sums(f):
                pe.wait_ge(y_stats, IMG_R * (f + 1))
                mm(conv_ps[:, 0, 0:3 * IMG_R], same_channel[:, :], sum_1[:, :, :].rearrange("p a m -> p (a m)"),
                   True, True).then_inc(y_stats_ps, 1)

            def conv(f, m):
                n = IMG_R * f + m
                hold(pe, x_normed, n + 1)
                if isinstance(n, int) and n == 0:
                    pe.wait_ge(x_normed_act, 1)
                hold(pe, w_mid_ready, f + 1)
                for b in range(2):
                    if not (isinstance(f, int) and f == 0 and m == 0):
                        hold(pe, x1_done, 2 * n - 1 + b)
                    for i, kx in enumerate((0, 2, 1)):
                        wk = w_mid[:, m, :] if kx == 1 else w_taps[:, kx, :]
                        rows_ = slice(b * GR // 2, (b + 1) * GR // 2)
                        for half, src in enumerate((xa[:, m], b_part(f, m))):
                            part = slice(half * P // 2, (half + 1) * P // 2)
                            last = mm(conv_ps[part, b, :], wk[:, part], src[:, rows_, kx:kx + W], i == 0, i == 2, True)
                    last.then_inc(conv_done, 1)

            def correlate(f, s):
                pe.wait_ge(z_done, IMG_R * f + 2 * s + 2)
                if not (isinstance(f, int) and f == 0):
                    pe.wait_ge(h_read[s], STEPS * f)
                for t in range(TILES):
                    zt = z[:, 2 * s + t // 2, t % 2 * HALF:(t % 2 + 1) * HALF].rearrange("p (n c) -> p c n", c=PATCH)
                    for c in range(PATCH):
                        last = mm(h[s][:, t, :], zt[:, c, :], d_sb[:, c, :], t % 2 == 0 and c == 0, c == PATCH - 1, True)
                    if t % 2:
                        last.then_inc(h_ready[s], 1)

            def update(r, s, k):
                pe.wait_ge(rows_in[s][k], 16 * TILES * (r + 1))
                for t in range(TILES):
                    pe.wait_ge(diag_ready[s], TILES * (r * (STEPS - 1) + k) + t + 1)
                    for j in range(k + 1):
                        last = mm(h[s][:, t, :], diag[s][:, t, j, :], rows[s][:, j, t, :], False, j == k, True)
                    if t % 2:
                        last.then_inc(h_ready[s], 1)

            def coef_transposes(r, m, dst=back_ps[0]):
                n = IMG_R * r + m
                by_dve = m - 1 if dst is final_ps and m >= 2 else 0
                pe.wait_ge(coef_ready, 2 * n + 2 - by_dve)
                if by_dve:
                    pe.wait_ge(coef_ready_dve, by_dve)
                if dst is back_ps[0]:
                    pe.wait_ge(y_done, 2 * n + 2)
                for k in range(CHUNKS):
                    for t in range(2):
                        last = nc.tensor.transpose(dst[:, k, t * P:(t + 1) * P],
                                                   picked[:, m % 2, t, 0, k * P:(k + 1) * P], ident[:, :])
                last.then_inc(coef_t_ps, 1)

            def reconstruct(r, m, final=False):
                n = IMG_R * r + m
                for q, half in enumerate((1, 0)):
                    if final:
                        pe.wait_ge(y_done, 2 * n + q + 1)
                    for c2 in range(2):
                        c = 2 * half + c2
                        if isinstance(n, int):
                            res = x1[:, n, c:PIX:PATCH]
                        else:
                            res = x1[:, bass.ds(n, 1), c:PIX:PATCH].rearrange("p a n -> p (a n)")
                        mm(back_ps[half][:, c2, :], ident[:, :], res, c2 == 0, False, True)
                    if q == 0:
                        pe.wait_ge(coef_t_done, n + 1)
                    for c2 in range(2):
                        for k in range(CHUNKS):
                            last = mm(back_ps[half][:, c2, :], d_t[:, k, 2 * half + c2, :], coef_t[:, k, :], False,
                                      k == CHUNKS - 1, True)
                    last.then_inc(recon_ps, 1)

            for m in range(IMG_R):
                conv(0, m)
            transpose_atoms()
            y_sums(0)
            gram_matrix()
            correlate(0, 0)
            pe.wait_ge(gram_sb_done, 1)
            pe.wait_ge(d_t_done, 1)

            def body(r, front, behind):
                f = r + 1
                b = r - 1
                correlate(r, 1)
                if front:
                    x_sums(f)
                if behind:
                    coef_transposes(b, 0)
                    reconstruct(b, 0)
                update(r, 0, 0)
                update(r, 1, 0)
                if front:
                    conv(f, 0)
                update(r, 0, 1)
                if behind:
                    coef_transposes(b, 1)
                if front:
                    conv(f, 1)
                update(r, 1, 1)
                if front:
                    conv(f, 2)
                update(r, 0, 2)
                if front:
                    conv(f, 3)
                update(r, 1, 2)
                if behind:
                    reconstruct(b, 1)
                if front:
                    y_sums(f)
                update(r, 0, 3)
                if behind:
                    coef_transposes(b, 2)
                    reconstruct(b, 2)
                update(r, 1, 3)
                if behind:
                    coef_transposes(b, 3)
                    reconstruct(b, 3)
                if front:
                    correlate(f, 0)

            body(0, True, False)
            with pe.Fori(1, ROUNDS - 1) as r:
                body(r, True, True)
            body(ROUNDS - 1, False, True)
            for m in range(IMG_R):
                coef_transposes(ROUNDS - 1, m, final_ps)
                reconstruct(ROUNDS - 1, m, True)

        @block.scalar
        def _(act):
            act.wait_ge(gate_loaded, 16)
            nc.scalar.activation(gate[:, 1:2], gate[:, 0:1], ACT.Sigmoid).then_inc(gate_done, 1)
            act.wait_ge(gate_done, 1)
            nc.scalar.activation(gate[:, 2:3], gate[:, 1:2], ACT.Sqrt)

            def x_statistics(f, m, unread=unread):
                hold(act, xa_loaded[m], 16 * 2 * (f + 1))
                for i, func in enumerate((ACT.Copy, ACT.Square)):
                    n = 2 * m + i
                    if n >= 3:
                        hold(act, x_stats, 2 * IMG_R * f + n - 2)
                    nc.scalar.activation(unread[:, n % 3], xa[:, m, :, 1:W + 1], func,
                                         accum_out=sum_x[:, i, m:m + 1]).then_inc(x_stats, 1)

            def root(ready, done, which, f):
                act.wait_ge(ready, f + 1)
                nc.scalar.activation(gn[:, which, 5, :], gn[:, which, 4, :], ACT.Sqrt).then_inc(done, 1)

            def norm_x(f, m):
                if m == 0:
                    act.wait_ge(x_params, f + 1)
                act.wait_ge(xb_loaded[m % 2], 16 * 2 * (2 * f + m // 2))
                bias, scale = gn[:, 0, 9, m:m + 1], gn[:, 0, 8, m:m + 1]
                for part in image_parts(f, m):
                    n_part = part.shape[0]
                    last = nc.scalar.activation(part, part, ACT.Identity, bias=bias[0:n_part], scale=scale[0:n_part])
                last.then_inc(x_normed, 1)

            def image_of(t, n):
                return t[:, n, :] if isinstance(n, int) else t[:, bass.ds(n, 1), :].rearrange("p a n -> p (a n)")

            def out_conv(f, m):
                n = IMG_R * f + m
                for b in range(2):
                    hold(act, conv_done, 2 * n + 1 + b)
                    nc.scalar.activation(image_of(x1, n)[:, b * HALF:(b + 1) * HALF], conv_ps[:, b, :], ACT.Identity,
                                         bias=gn[:, 0, 10, m:m + 1], accum_out=sum_1[:, b, m:m + 1]).then_inc(x1_done, 1)

            def square_sum(f, m):
                n = IMG_R * f + m
                hold(act, x1_done, 2 * n + 2)
                nc.scalar.activation(z[:, m, :], image_of(x1, n), ACT.Square, accum_out=sum_1[:, 2, m:m + 1]
                                     ).then_inc(y_stats, 1)

            def norm_y(f, m):
                n = IMG_R * f + m
                if m == 0:
                    hold(act, y_params, f + 1)
                nc.scalar.activation(z[:, m, :], image_of(x1, n), ACT.Identity,
                                     bias=gn[:, 1, 9, m:m + 1], scale=gn[:, 1, 8, m:m + 1]).then_inc(z_done, 1)

            def scores(r, s, k):
                for b in range(2):
                    act.wait_ge(h_ready[s], 2 * (STEPS * r + k) + b + 1)
                    if b == 0 and not (isinstance(r, int) and r == 0 and k == 0):
                        act.wait_ge(h_read[s], STEPS * r + k)
                    nc.scalar.activation(score[s][:, 2 * b:2 * b + 2, :], h[s][:, 2 * b:2 * b + 2, :], ACT.Abs
                                         ).then_inc(score_ready[s], 1)

            def diags(r, s, k):
                act.wait_ge(dx_ready[s], (STEPS - 1) * r + k + 1)
                if not (isinstance(r, int) and r == 0 and k == 0):
                    act.wait_ge(h_ready[s], 2 * (STEPS * r + k) + 2)
                for t in range(TILES):
                    for j in range(k + 1):
                        last = nc.scalar.activation(diag[s][:, t, j, :], ident[:, :], ACT.Copy, scale=dx[s][:, t, j:j + 1])
                    last.then_inc(diag_ready[s], 1)

            def copy_coef(r, m, src=back_ps[0]):
                n = IMG_R * r + m
                act.wait_ge(coef_t_ps, n + 3)
                nc.scalar.activation(coef_t[:, :, :], src[:, :, :], ACT.Copy, scale=-1.0).then_inc(coef_t_done, 1)

            def out_back(r, m):
                n = IMG_R * r + m
                dst = image_of(x1, n).rearrange("p (n c) -> p c n", c=PATCH)
                for q, half in enumerate((1, 0)):
                    hold(act, recon_ps, 2 * n + q + 1)
                    nc.scalar.activation(dst[:, 2 * half:2 * half + 2, :], back_ps[half][:, :, :], ACT.Copy).then_inc(y_done, 1)

            act.sem_inc(y_done, 2)
            act.wait_ge(pads_zero, 1)
            for m in range(IMG_R):
                x_statistics(0, m)
            act.wait_ge(d_loaded, 16 * PATCH)
            nc.scalar.activation(d_tmp[:, :, :], d_sb[:, :, :], ACT.Square).then_inc(d_sq, 1)
            root(x_var, x_root, 0, 0)
            act.wait_ge(x_params, 1)
            act.wait_ge(xb_loaded[0], 16 * 2)
            for part in image_parts(0, 0)[1::2]:
                n_part = part.shape[0]
                last = nc.scalar.activation(part, part, ACT.Identity, bias=gn[0:n_part, 0, 9, 0:1],
                                            scale=gn[0:n_part, 0, 8, 0:1])
            last.then_inc(x_normed_act, 1)
            act.wait_ge(d_nrm, 1)
            nc.scalar.activation(d_norm[:, 1, :], d_norm[:, 0, :], ACT.Sqrt).then_inc(d_root, 1)
            for m in range(IMG_R):
                out_conv(0, m)
                if m not in DVE_SQUARES:
                    square_sum(0, m)
                if m == 1:
                    x_statistics(1, 0, unread_first)
            root(y_var, y_root, 1, 0)
            act.wait_ge(d_t_ps, 1)
            for k in range(CHUNKS):
                last = nc.scalar.activation(d_t[:, k, :, :].rearrange("p c n -> p (c n)"),
                                            back_ps[k][:, :, :].rearrange("p a n -> p (a n)"), ACT.Copy)
            last.then_inc(d_t_done, 1)
            x_statistics(1, 1, unread_first)
            x_statistics(1, 2, unread_first)
            scores(0, 0, 0)
            x_statistics(1, 3, unread_first)

            def body(r, front, behind):
                f = r + 1
                b = r - 1
                if front and behind:
                    for m in range(IMG_R):
                        x_statistics(f, m)
                scores(r, 1, 0)
                if behind:
                    copy_coef(b, 0)
                if front:
                    root(x_var, x_root, 0, f)
                diags(r, 0, 0)
                if behind:
                    out_back(b, 0)
                if front:
                    norm_x(f, 0)
                scores(r, 0, 1)
                if front:
                    norm_x(f, 1)
                diags(r, 1, 0)
                scores(r, 1, 1)
                diags(r, 0, 1)
                if front:
                    out_conv(f, 0)
                scores(r, 0, 2)
                if front:
                    square_sum(f, 0)
                if behind:
                    copy_coef(b, 1)
                if front:
                    norm_x(f, 2)
                diags(r, 1, 1)
                if front:
                    out_conv(f, 1)
                scores(r, 1, 2)
                if front:
                    square_sum(f, 1)
                if front:
                    norm_x(f, 3)
                diags(r, 0, 2)
                if front:
                    out_conv(f, 2)
                scores(r, 0, 3)
                if front:
                    square_sum(f, 2)
                diags(r, 1, 2)
                if front:
                    out_conv(f, 3)
                scores(r, 1, 3)
                if front:
                    square_sum(f, 3)
                if behind:
                    out_back(b, 1)
                diags(r, 0, 3)
                if front:
                    root(y_var, y_root, 1, f)
                scores(r, 0, 4)
                if behind:
                    copy_coef(b, 2)
                diags(r, 1, 3)
                if front:
                    norm_y(f, 0)
                    norm_y(f, 1)
                if behind:
                    out_back(b, 2)
                scores(r, 1, 4)
                if behind:
                    copy_coef(b, 3)
                if front:
                    norm_y(f, 2)
                    norm_y(f, 3)
                if behind:
                    out_back(b, 3)
                if front:
                    scores(f, 0, 0)

            body(0, True, False)
            with act.Fori(1, ROUNDS - 1) as r:
                body(r, True, True)
            body(ROUNDS - 1, False, True)
            for m in range(IMG_R):
                copy_coef(ROUNDS - 1, m, final_ps)
                out_back(ROUNDS - 1, m)

        @block.vector
        def _(dve):
            v = nc.vector
            n = 0

            def step(ins):
                nonlocal n
                n += 1
                ins.then_inc(dve_step, 1)
                return n

            def after(count):
                dve.wait_ge(dve_step, count)

            def sync():
                after(n)

            def restart():
                nonlocal n
                sync()
                dve.sem_clear(dve_step)
                n = 0

            for t in (xa, xb, xb_first):
                step(v.memset(t[:, :, :, 0:1], 0.0))
                step(v.memset(t[:, :, :, W + 1:W + 2], 0.0))
            sync()
            for m in range(IMG_R):
                step(v.memset(xa[3 * C:4 * C, m, 0, :], 0.0))
                step(v.memset(xa[0:3 * C, m, GR, :], 0.0))
            for m in range(2):
                step(v.memset(xb[3 * C:4 * C, m, GR - 1, :], 0.0))
                step(v.memset(xb_first[3 * C:4 * C, m, GR - 1, :], 0.0))
            sync()
            dve.sem_inc(pads_zero, 1)
            for c in range(8):
                step(v.memset(rank[:, c:c + 1], 1024.0 * (8 - c)))
            for s in range(2):
                step(v.memset(n_inv[s][:, :, :, :], 0.0))
                step(v.memset(rd[s][:, :, :], 1.0))
            sync()
            for s in range(2):
                for k in range(STEPS):
                    step(v.memset(n_inv[s][:, :, k, k:k + 1], 1.0))
            step(v.memset(w_taps[:, :, :], 0.0))

            def together(*parts):
                parts = list(parts)
                while parts:
                    for part in list(parts):
                        if next(part, parts) is parts:
                            parts.remove(part)
                        else:
                            yield

            def run(*parts):
                for _ in together(*parts):
                    pass

            def variance(f, which, sums, done):
                g = gn[:, which]
                dve.wait_ge(sums, f + 1)
                first = 1 - which
                c = step(v.tensor_scalar(g[:, first:3, :].rearrange("p a m -> p (a m)"),
                                         conv_ps[:, 0, 0:(3 - first) * IMG_R], 1.0 / (H * W), None, ALU.mult))
                yield
                if which:
                    after(c)
                    c = step(v.tensor_tensor(g[:, 1, :], g[:, 0, :], g[:, 1, :], ALU.add))
                    yield
                after(c)
                c = step(v.tensor_tensor(g[:, 3, :], g[:, 1, :], g[:, 1, :], ALU.mult))
                yield
                after(c)
                c = step(v.tensor_tensor(g[:, 3, :], g[:, 2, :], g[:, 3, :], ALU.subtract))
                yield
                after(c)
                v.tensor_scalar(g[:, 4, :], g[:, 3, :], 0.0, GN_EPS, ALU.max, ALU.add).then_inc(done, 1)

            def norm_params(f, which, root_done, done):
                g = gn[:, which]
                dve.wait_ge(root_done, f + 1)
                c = step(v.reciprocal(g[:, 6, :], g[:, 5, :]))
                yield
                after(c)
                c = step(v.tensor_tensor(g[:, 6, :], g[:, 6, :], g[:, 4, :], ALU.mult))
                yield
                after(c)
                c = step(v.tensor_tensor(g[:, 7, :], g[:, 5, :], g[:, 6, :], ALU.add))
                yield
                after(c)
                c = step(v.tensor_scalar(g[:, 7, :], g[:, 7, :], 0.5, None, ALU.mult))
                yield
                after(c)
                c = step(v.reciprocal(g[:, 8, :], g[:, 7, :]))
                c2 = step(v.tensor_scalar(g[:, 10, :], g[:, 1, :], b_eff[:, 0:1], None, ALU.add))
                yield
                after(c)
                c = step(v.scalar_tensor_tensor(out=g[:, 9, :], in0=g[:, 1, :], scalar=-1.0, in1=g[:, 8, :],
                                                op0=ALU.mult, op1=ALU.mult))
                yield
                after(c)
                dve.sem_inc(done, 1)
                if which == 0:
                    for m in range(IMG_R):
                        c = step(v.scalar_tensor_tensor(out=w_mid[:, m, :], in0=center[:, :], scalar=gn[:, 0, 7, m:m + 1],
                                                        in1=w_taps[:, 1, :], op0=ALU.mult, op1=ALU.add))
                        yield
                    after(c)
                    dve.sem_inc(w_mid_ready, 1)

            picked_g = [0, 0]
            picked_h = [0, 0]

            def all_picked(s):
                after(picked_h[s])
                dve.sem_inc(h_read[s], 1)

            def scan(r, s, k, other=iter(()), read=None):
                first = []
                for t in range(TILES):
                    if t % 2 == 0:
                        hold(dve, score_ready[s], 2 * (STEPS * r + k) + t // 2 + 1)
                    first.append(step(v.max(out=top[s][:, t, :], in_=score[s][:, t, :])))
                    if t == 0 and read is not None:
                        all_picked(read)
                    next(other, None)
                for t in range(TILES):
                    after(first[t])
                    step(v.max_index(out=top_i[s][:, t, :], in_max=top[s][:, t, :], in_values=score[s][:, t, :]))
                    next(other, None)
                    next(other, None)
                for _ in other:
                    pass

            def select(r, s, k, other=iter(())):
                sync()
                if k == 0:
                    step(v.memset(x_neg[s][:, :, 1:STEPS], 0.0))
                    c = step(v.tensor_copy(idx_u[s][:, 0, :], top_i[s][:, :, 0]))
                else:
                    by_rank = rank[:, :].rearrange("p (a c) -> p a c", a=1).to_broadcast([P, TILES, 8])
                    if k == 1:
                        old = idx_u[s][:, 0, :].rearrange("p (t a) -> p t a", a=1)
                        step(v.tensor_tensor(keep[s][:, :, :], top_i[s][:, :, :],
                                             old.to_broadcast([P, TILES, 8]), ALU.not_equal))
                        c = step(v.tensor_tensor(enc[s][:, :, :], top_i[s][:, :, :], by_rank, ALU.add))
                        next(other, None)
                    else:
                        i8 = top_i[s][:, :, :].rearrange("p t (c a) -> p t c a", a=1).to_broadcast([P, TILES, 8, k])
                        old = idx_u[s][:, 0:k, :].rearrange("p j (t a) -> p t a j", a=1).to_broadcast([P, TILES, 8, k])
                        c = step(v.tensor_tensor(free[s][:, :, :, 0:k], i8, old, ALU.not_equal))
                        step(v.tensor_tensor(enc[s][:, :, :], top_i[s][:, :, :], by_rank, ALU.add))
                        after(c)
                        c = step(v.tensor_reduce(keep[s][:, :, :], free[s][:, :, :, 0:k], AX.X, ALU.min))
                        next(other, None)
                    after(c)
                    c = step(v.tensor_tensor(enc[s][:, :, :], enc[s][:, :, :], keep[s][:, :, :], ALU.mult))
                    next(other, None)
                    after(c)
                    c = step(v.tensor_reduce(best[s][:, :], enc[s][:, :, :], AX.X, ALU.max))
                    next(other, None)
                    after(c)
                    c = step(v.tensor_scalar(idx_u[s][:, k, :], best[s][:, :], 1023, None, ALU.bitwise_and))
                    next(other, None)
                    next(other, None)
                after(c)
                if k < STEPS - 1:
                    dve.sem_inc(idx_ready[s], 1)
                else:
                    step(v.tensor_copy(idx_last[s][:, :, :], idx_u[s][:, :, :].rearrange("p j t -> p t j")))

            junk_n = [0]

            def pick(s, t, k, source, dst):
                if junk_n[0] >= JUNK:
                    after(junk_c[junk_n[0] % JUNK])
                place = junk[:, junk_n[0] % JUNK, :]
                if k < MASKED:
                    c = step(v.scalar_tensor_tensor(out=place, in0=iota[:, :], scalar=idx_u[s][:, k, t:t + 1],
                                                    in1=source, op0=ALU.is_equal, op1=ALU.mult, accum_out=dst))
                else:
                    c = step(v.scalar_tensor_tensor(out=place, in0=mask[:, t, :], scalar=1.0,
                                                    in1=source, op0=ALU.mult, op1=ALU.mult, accum_out=dst))
                junk_c[junk_n[0] % JUNK] = c
                junk_n[0] += 1

            junk_c = [0] * JUNK

            def extract(r, s, k, chain, other=iter(())):
                marked = []
                if k >= MASKED:
                    for t in range(TILES):
                        marked.append(step(v.tensor_scalar(mask[:, t, :], iota_short[:, :], idx_u[s][:, k, t:t + 1], None,
                                                           ALU.is_equal)))
                for j in range(k):
                    if j == k - 1:
                        dve.wait_ge(rows_in[s][j], 16 * TILES * (r + 1))
                    for t in range(TILES):
                        if j == 0 and marked:
                            after(marked[t])
                        pick(s, t, k, rows[s][:, j, t, :], g_at[s][:, t, j:j + 1])
                        next(other, None)
                picked_g[s] = n
                for t in range(TILES):
                    pick(s, t, k, h[s][:, t, :], h_at[s][:, t:t + 1])
                    next(other, None)
                    if k > 0:
                        next(chain)
                picked_h[s] = n
                for _ in other:
                    pass

            def solve(r, s, k):
                T = TILES
                if k > 0:
                    after(picked_g[s])
                    g_b = g_at[s][:, :, 0:k].rearrange("p t (a j) -> p t a j", a=1).to_broadcast([P, T, k, k])
                    c = step(v.tensor_tensor(prod[s][:, :, 0:k, 0:k], n_inv[s][:, :, 0:k, 0:k], g_b, ALU.mult))
                    yield
                    after(c)
                    c = step(v.tensor_reduce(w_vec[s][:, :, 0:k], prod[s][:, :, 0:k, 0:k], AX.X, ALU.add))
                    yield
                    after(c)
                    c = step(v.tensor_tensor(a_vec[s][:, :, 0:k], w_vec[s][:, :, 0:k], rd[s][:, :, 0:k], ALU.mult))
                    yield
                    after(c)
                    c = step(v.tensor_tensor(aw[s][:, :, 0:k], a_vec[s][:, :, 0:k], w_vec[s][:, :, 0:k], ALU.mult))
                    a_b = a_vec[s][:, :, 0:k].rearrange("p t (a i) -> p t a i", a=1).to_broadcast([P, T, k, k])
                    c2 = step(v.tensor_tensor(prod[s][:, :, 0:k, 0:k],
                                              n_inv[s][:, :, 0:k, 0:k].rearrange("p t i j -> p t j i"), a_b, ALU.mult))
                    yield
                    after(c)
                    c = step(v.tensor_reduce(d_neg[s][:, :], aw[s][:, :, 0:k], AX.X, ALU.add, negate=True))
                    after(c2)
                    c2 = step(v.tensor_reduce(n_inv[s][:, :, k, 0:k], prod[s][:, :, 0:k, 0:k], AX.X, ALU.add, negate=True))
                    yield
                    after(c)
                    c = step(v.tensor_scalar(d_k[s][:, :], d_neg[s][:, :], 1.0, DIAG_EPS, ALU.add, ALU.max))
                    yield
                    after(c)
                    c = step(v.reciprocal(rd[s][:, :, k], d_k[s][:, :]))
                    yield
                    after(c)
                after(picked_h[s])
                c = step(v.scalar_tensor_tensor(out=c_neg[s][:, :], in0=h_at[s][:, :], scalar=-1.0, in1=rd[s][:, :, k],
                                                op0=ALU.mult, op1=ALU.mult))
                yield
                after(c)
                c_b = c_neg[s][:, :].rearrange("p (t a) -> p t a", a=1).to_broadcast([P, T, k + 1])
                c = step(v.tensor_tensor(dx[s][:, :, 0:k + 1], n_inv[s][:, :, k, 0:k + 1], c_b, ALU.mult))
                yield
                after(c)
                if k < STEPS - 1:
                    dve.sem_inc(dx_ready[s], 1)
                if k == 0:
                    step(v.tensor_copy(x_neg[s][:, :, 0], dx[s][:, :, 0]))
                else:
                    total = x_neg[s] if k < STEPS - 1 else x_last[s]
                    step(v.tensor_tensor(total[:, :, 0:k + 1], x_neg[s][:, :, 0:k + 1], dx[s][:, :, 0:k + 1], ALU.add))

            def scatter(r, m):
                hold(dve, coef_t_ps, IMG_R * r + m + 1)
                for t in range(2):
                    tile = 2 * (m % 2) + t
                    for j in range(STEPS):
                        c = step(v.tensor_scalar(picked[:, m % 2, t, j, :], iota[:, :], idx_last[m // 2][:, tile, j:j + 1],
                                                 x_last[m // 2][:, tile, j:j + 1], ALU.is_equal, ALU.mult))
                        yield
                    after(c)
                    dve.sem_inc(picked_ready, 1)

            dve.wait_ge(w_loaded, 16 * 4)
            step(v.tensor_reduce(w_sum[:, :], w_raw[:, :, :], AX.X, ALU.add, apply_absolute_value=True))
            sync()
            dve.sem_inc(w_sum_ready, 1)
            dve.wait_ge(w_sum_ps, 1)
            step(v.tensor_scalar(w_scale[:, 0:2], conv_ps[:, 0, 0:2], 1.0 / (PATCH * C * C * TAPS), SCALE_EPS, ALU.mult, ALU.max))
            sync()
            step(v.tensor_scalar(w_scale[:, 2:4], w_scale[:, 0:2], 0.5, None, ALU.mult))
            dve.wait_ge(gate_done, 1)
            sync()
            for i in range(2):
                step(v.tensor_scalar(w_tmp[:, 0, :], w_raw[:, i, :], w_scale[:, 2 + i:3 + i], w_scale[:, i:i + 1], ALU.is_gt, ALU.mult))
                step(v.tensor_scalar(w_tmp[:, 1, :], w_raw[:, i, :], -1.0, w_scale[:, 2 + i:3 + i], ALU.mult, ALU.is_gt))
                sync()
                step(v.tensor_scalar(w_tmp[:, 1, :], w_tmp[:, 1, :], w_scale[:, i:i + 1], None, ALU.mult))
                sync()
                step(v.tensor_tensor(w_raw[:, i, :], w_tmp[:, 0, :], w_tmp[:, 1, :], ALU.subtract))
                sync()
            step(v.scalar_tensor_tensor(out=w_tmp[:, 2, :], in0=w_raw[:, 1, :], scalar=gate[:, 1:2], in1=w_raw[:, 0, :],
                                        op0=ALU.mult, op1=ALU.add))
            step(v.scalar_tensor_tensor(out=b_eff[:, :], in0=b_raw[:, 1:2], scalar=gate[:, 1:2], in1=b_raw[:, 0:1],
                                        op0=ALU.mult, op1=ALU.add))
            sync()
            for tap in range(TAPS):
                step(v.transpose(w_t[:, tap, :], w_tmp[:, 2, :].rearrange("p (i t) -> p t i", t=TAPS)[:, tap, :]))
            sync()
            for p in range(PATCH):
                held_rows = (0, 1, 2, -1) if p < 2 else (1, 2, 3, 4)
                for q in range(PATCH):
                    ky = held_rows[q] - p + 1
                    if 0 <= ky < 3:
                        part = slice(q * C, (q + 1) * C)
                        step(v.tensor_copy(w_taps[part, :, p * C:(p + 1) * C], w_t[part, 3 * ky:3 * ky + 3, :]))
            sync()
            dve.sem_inc(w_ready, 1)
            dve.wait_ge(const_done, 1)
            run(variance(0, 0, x_stats_ps, x_var))
            run(norm_params(0, 0, x_root, x_params))

            def apply_norm_x(m):
                if m > 0:
                    dve.wait_ge(xb_loaded[m] if m < 2 else xb_first_loaded[m - 2], 16 * 2)
                for part in image_parts(0, m) if m > 0 else image_parts(0, 0)[0::2]:
                    n_part = part.shape[0]
                    c = step(v.tensor_scalar(part, part, gn[0:n_part, 0, 8, m:m + 1], gn[0:n_part, 0, 9, m:m + 1],
                                             ALU.mult, ALU.add))
                after(c)
                dve.sem_inc(x_normed, 1)

            apply_norm_x(0)
            dve.wait_ge(d_sq_ps, 1)
            step(v.tensor_copy(d_norm[:, 0, :], back_ps[0][:, 0, :]))
            sync()
            dve.sem_inc(d_nrm, 1)
            apply_norm_x(1)
            dve.wait_ge(d_root, 1)
            step(v.reciprocal(d_norm[:, 2, :], d_norm[:, 1, :]))
            sync()
            step(v.tensor_tensor(d_norm[:, 3, :], d_norm[:, 2, :], d_norm[:, 0, :], ALU.mult))
            sync()
            step(v.tensor_tensor(d_norm[:, 2, :], d_norm[:, 3, :], d_norm[:, 1, :], ALU.add))
            sync()
            step(v.tensor_scalar(d_norm[:, 3, :], d_norm[:, 2, :], 0.5, NORM_EPS, ALU.mult, ALU.add))
            sync()
            step(v.reciprocal(d_norm[:, 2, :], d_norm[:, 3, :]))
            sync()
            for c in range(PATCH):
                step(v.tensor_tensor(d_sb[:, c, :], d_sb[:, c, :], d_norm[:, 2, :], ALU.mult))
            sync()
            dve.sem_inc(d_ready, 1)
            apply_norm_x(2)
            apply_norm_x(3)
            for m in DVE_SQUARES:
                dve.wait_ge(x1_done, 2 * m + 2)
                c = step(v.scalar_tensor_tensor(out=z[:, m, :], in0=x1[:, m, :], scalar=1.0, in1=x1[:, m, :],
                                                op0=ALU.mult, op1=ALU.mult, accum_out=sum_1[:, 2, m:m + 1]))
                after(c)
                dve.sem_inc(y_stats, 1)
            run(variance(0, 1, y_stats_ps, y_var))
            run(norm_params(0, 1, y_root, y_params))
            for m in range(IMG_R):
                c = step(v.tensor_scalar(z[:, m, :], x1[:, m, :], gn[:, 1, 8, m:m + 1], gn[:, 1, 9, m:m + 1],
                                         ALU.mult, ALU.add))
                after(c)
                dve.sem_inc(z_done, 1)
            dve.wait_ge(gram_ps, 1)
            for k in range(CHUNKS):
                step(v.tensor_copy(gram[:, k, :], h[1][:, 2 * k, :]))
            sync()
            for k in range(CHUNKS):
                step(v.scalar_tensor_tensor(out=gram[:, k, k * P:(k + 1) * P], in0=ident[:, :], scalar=DIAG_EPS,
                                            in1=gram[:, k, k * P:(k + 1) * P], op0=ALU.mult, op1=ALU.add))
            sync()
            dve.sem_inc(gram_sb_done, 1)

            def body(r, front, behind):
                f = r + 1
                restart()
                junk_n[0] = 0
                nothing = iter(())
                chain = [nothing, nothing]
                for k in range(STEPS):
                    rows_of = scatter(r - 1, k + 1) if behind and k in (1, 2) else nothing
                    beside = [nothing] * 4
                    if front and k == 0:
                        beside[1] = variance(f, 0, x_stats_ps, x_var)
                        beside[2] = norm_params(f, 0, x_root, x_params)
                    if front and k == 3:
                        beside[3] = variance(f, 1, y_stats_ps, y_var)
                    if front and k == 4:
                        beside[0] = norm_params(f, 1, y_root, y_params)
                    if k:
                        scan(r, 0, k, together(chain[1], beside[0]), 1)
                    else:
                        scan(r, 0, k)
                    select(r, 0, k, rows_of)
                    chain[0] = solve(r, 0, k)
                    extract(r, 0, k, chain[0], beside[1])
                    scan(r, 1, k, together(chain[0], beside[2]), 0)
                    if k == STEPS - 1:
                        rows_of = scatter(r, 0)
                    select(r, 1, k, rows_of)
                    if not front and k == STEPS - 1:
                        run(rows_of)
                        run(scatter(r, 1))
                    if k < STEPS - 1:
                        run(rows_of)
                    chain[1] = solve(r, 1, k)
                    extract(r, 1, k, chain[1], beside[3])
                all_picked(1)
                run(chain[1], rows_of)
                if front:
                    run(scatter(r, 1))

            body(0, True, False)
            with dve.Fori(1, ROUNDS - 1) as r:
                body(r, True, True)
            body(ROUNDS - 1, False, True)
            sync()
            for m in range(2, IMG_R):
                run(scatter(ROUNDS - 1, m))
                for j in range(1, STEPS):
                    c = step(v.tensor_tensor(picked[:, m % 2, 1, 0, :], picked[:, m % 2, 1, 0, :],
                                             picked[:, m % 2, 1, j, :], ALU.add))
                    after(c)
                dve.sem_inc(coef_ready_dve, 1)


_INS = ['x', 'L0_conv_w', 'L0_conv_b', 'L0_conv_w_child', 'L0_conv_b_child', 'L0_conv_gate', 'L1_conv_dictionary']


def kernel(**inputs):
    import numpy as _np
    import concourse.bacc as _bacc
    from concourse import mybir as _mybir
    from concourse.bass_utils import run_bass_kernel_spmd as _run

    nc = _bacc.Bacc("TRN2", target_bir_lowering=False, num_devices=1)
    arrays, args = {}, []
    for name in _INS:
        a = _np.ascontiguousarray(inputs[name])
        arrays[f"in_{name}"] = a
        args.append(nc.dram_tensor(f"in_{name}", a.shape, _mybir.dt.from_np(a.dtype), kind="ExternalInput").ap())
    result = nc.dram_tensor("out_0", inputs['x'].shape, _mybir.dt.float32, kind="ExternalOutput").ap()
    build_program(nc, *args, result)
    r = _run(nc, [arrays], core_ids=[0])
    return r.results[0]["out_0"]
```
